# Optimizing a Trainium2 kernel written in Bass

```python
import numpy as np
import jax
import jax.numpy as jnp

def _softmax(x, axis=-1):
    return jax.nn.softmax(x, axis=axis)

def _gelu(x):
    return jax.nn.gelu(x, approximate=True)

def _silu(x):
    return jax.nn.silu(x)

def _sigmoid(x):
    return jax.nn.sigmoid(x)

def _layernorm(x, axis=-1, eps=1e-05):
    m = jnp.mean(x, axis=axis, keepdims=True)
    v = jnp.var(x, axis=axis, keepdims=True)
    return (x - m) / jnp.sqrt(v + eps)

def _scatter_add(tgt, idx, src, axis=0):
    return tgt.at[idx].add(src)

def _segment_sum(src, seg, n):
    return jax.ops.segment_sum(src, seg, n)
kernel_name = 'mk_hybrid_d1_jaxref_r8_67dea5'

def setup_inputs(seed: int=0):
    np.random.seed(seed)
    _w = jnp.asarray

    def _L0_attn_a_setup():
        import jax, jax.numpy as jnp
        import numpy as np
        B, L, D_MODEL = (4, 256, 128)
        D_STATE = 64
        EXPAND = 2
        D_INNER = EXPAND * D_MODEL
        EPS = 1e-05

        def _s6_forward(x, Wi, bi, Wx, bx, Wdt, bdt, A_log, Dp, Wo, bo, gamma, beta):
            residual = x
            x_and_res = x @ Wi + bi
            xs, res = jnp.split(x_and_res, [D_INNER], axis=-1)
            xs = jax.nn.silu(xs)
            x_dbl = xs @ Wx + bx
            d_raw = x_dbl[..., :D_STATE]
            B_sel = x_dbl[..., D_STATE:2 * D_STATE]
            C_sel = x_dbl[..., 2 * D_STATE:]
            delta = jax.nn.softplus(d_raw @ Wdt + bdt)
            A = -jnp.exp(A_log.astype(jnp.float32))

            def step(h, t):
                delta_t, B_t, x_t, C_t = t
                dA = jnp.exp(delta_t[..., None] * A)
                dB = delta_t[..., None] * B_t[:, None, :]
                h = dA * h + dB * x_t[..., None]
                y_t = C_t * jnp.sum(h, axis=-1)
                return (h, y_t)
            seq = (jnp.moveaxis(delta, 1, 0), jnp.moveaxis(B_sel, 1, 0), jnp.moveaxis(xs, 1, 0), jnp.moveaxis(C_sel, 1, 0))
            h0 = jnp.zeros((x.shape[0], D_INNER, D_STATE), x.dtype)
            _, y = jax.lax.scan(step, h0, seq)
            y = jnp.moveaxis(y, 0, 1)
            y = y + xs * Dp
            y = y * jax.nn.silu(res)
            out = y @ Wo + bo
            z = out + residual
            mu = jnp.mean(z, axis=-1, keepdims=True)
            var = jnp.mean((z - mu) ** 2, axis=-1, keepdims=True)
            return gamma * (z - mu) / jnp.sqrt(var + EPS) + beta
        key = jax.random.key(seed)
        ks = jax.random.split(key, 8)
        s = lambda fan_in: 1.0 / np.sqrt(fan_in)
        return {'x': jax.random.normal(ks[0], (B, L, D_MODEL), jnp.float32), 'Wi': jax.random.normal(ks[1], (D_MODEL, 2 * D_INNER), jnp.float32) * s(D_MODEL), 'bi': jnp.zeros((2 * D_INNER,), jnp.float32), 'Wx': jax.random.normal(ks[2], (D_INNER, 2 * D_STATE + D_INNER), jnp.float32) * s(D_INNER), 'bx': jnp.zeros((2 * D_STATE + D_INNER,), jnp.float32), 'Wdt': jax.random.normal(ks[3], (D_STATE, D_INNER), jnp.float32) * s(D_STATE), 'bdt': jnp.zeros((D_INNER,), jnp.float32), 'A_log': jax.random.uniform(ks[4], (D_INNER, D_STATE), jnp.float32, -4.0, -2.0), 'Dp': 1.0 + 0.1 * jax.random.normal(ks[5], (D_INNER,), jnp.float32), 'Wo': jax.random.normal(ks[6], (D_INNER, D_MODEL), jnp.float32) * s(D_INNER), 'bo': jnp.zeros((D_MODEL,), jnp.float32), 'gamma': jnp.ones((D_MODEL,), jnp.float32), 'beta': jnp.zeros((D_MODEL,), jnp.float32)}
    _L0_attn_a_in = _L0_attn_a_setup()

    def _L0_attn_b_setup():
        import jax, jax.numpy as jnp
        import numpy as np
        DT_MIN, DT_MAX = (0.001, 0.1)
        STEP_RESCALE = 1.0

        def _s5_forward(u, Lambda_re, Lambda_im, B, C, D, log_step):
            Lambda = jnp.minimum(Lambda_re, -0.0001) + 1j * Lambda_im
            B_tilde = (B[..., 0] + 1j * B[..., 1]).astype(jnp.complex64)
            C_tilde = (C[..., 0] + 1j * C[..., 1]).astype(jnp.complex64)
            step = STEP_RESCALE * jnp.exp(log_step[:, 0])
            Lambda_bar = jnp.exp(Lambda * step)
            B_bar = ((Lambda_bar - 1.0) / Lambda)[:, None] * B_tilde
            Bu = jnp.einsum('blh,ph->blp', u.astype(jnp.complex64), B_bar)
            A = jnp.broadcast_to(Lambda_bar, Bu.shape)

            def combine(e_i, e_j):
                a_i, b_i = e_i
                a_j, b_j = e_j
                return (a_j * a_i, a_j * b_i + b_j)
            _, xs = jax.lax.associative_scan(combine, (A, Bu), axis=1)
            ys = jnp.einsum('blp,hp->blh', xs, C_tilde).real + D * u
            return ys
        key = jax.random.key(seed)
        ks = jax.random.split(key, 7)
        Bsz, L, H, P = (8, 512, 128, 64)
        u = jax.random.normal(ks[0], (Bsz, L, H), jnp.float32)
        Lambda_re = -0.5 * jnp.abs(jax.random.normal(ks[1], (P,), jnp.float32)) - 0.1
        Lambda_im = jnp.pi * jax.random.normal(ks[2], (P,), jnp.float32)
        Bp = jax.random.normal(ks[3], (P, H, 2), jnp.float32) / np.sqrt(H)
        Cp = jax.random.normal(ks[4], (H, P, 2), jnp.float32) / np.sqrt(P)
        D = jax.random.normal(ks[5], (H,), jnp.float32)
        log_step = jnp.log(jax.random.uniform(ks[6], (P, 1), jnp.float32) * (DT_MAX - DT_MIN) + DT_MIN)
        return {'u': u, 'Lambda_re': Lambda_re, 'Lambda_im': Lambda_im, 'B': Bp, 'C': Cp, 'D': D, 'log_step': log_step}
    _L0_attn_b_in = _L0_attn_b_setup()

    def _L0_ffn_setup():
        import jax, jax.numpy as jnp
        import numpy as np
        E = 8
        TOP_K = 2
        DIM = 128
        HID = 256
        key = jax.random.key(seed)
        k1, k2, k3, k4, k5 = jax.random.split(key, 5)
        s = 0.02
        x = jax.random.normal(k1, (2, 256, DIM), dtype=jnp.float32)
        Wg = jax.random.normal(k2, (DIM, E), dtype=jnp.float32) * s
        W1 = jax.random.normal(k3, (E, DIM, HID), dtype=jnp.float32) * s
        W2 = jax.random.normal(k4, (E, DIM, HID), dtype=jnp.float32) * s
        W3 = jax.random.normal(k5, (E, HID, DIM), dtype=jnp.float32) * s
        return {'x': x, 'Wg': Wg, 'W1': W1, 'W2': W2, 'W3': W3}
    _L0_ffn_in = _L0_ffn_setup()
    _d = {'L0_attn_a_x': _L0_attn_a_in['x'], 'L0_attn_a_Wi': _L0_attn_a_in['Wi'], 'L0_attn_a_bi': _L0_attn_a_in['bi'], 'L0_attn_a_Wx': _L0_attn_a_in['Wx'], 'L0_attn_a_bx': _L0_attn_a_in['bx'], 'L0_attn_a_Wdt': _L0_attn_a_in['Wdt'], 'L0_attn_a_bdt': _L0_attn_a_in['bdt'], 'L0_attn_a_A_log': _L0_attn_a_in['A_log'], 'L0_attn_a_Dp': _L0_attn_a_in['Dp'], 'L0_attn_a_Wo': _L0_attn_a_in['Wo'], 'L0_attn_a_bo': _L0_attn_a_in['bo'], 'L0_attn_a_gamma': _L0_attn_a_in['gamma'], 'L0_attn_a_beta': _L0_attn_a_in['beta'], 'L0_attn_b_Lambda_re': _L0_attn_b_in['Lambda_re'], 'L0_attn_b_Lambda_im': _L0_attn_b_in['Lambda_im'], 'L0_attn_b_B': _L0_attn_b_in['B'], 'L0_attn_b_C': _L0_attn_b_in['C'], 'L0_attn_b_D': _L0_attn_b_in['D'], 'L0_attn_b_log_step': _L0_attn_b_in['log_step'], 'L0_ffn_Wg': _L0_ffn_in['Wg'], 'L0_ffn_W1': _L0_ffn_in['W1'], 'L0_ffn_W2': _L0_ffn_in['W2'], 'L0_ffn_W3': _L0_ffn_in['W3']}
    _x0 = _d['L0_attn_a_x']
    _d['L0_attn_a_x'] = jax.random.normal(jax.random.fold_in(jax.random.key(seed), 1), (8, 512, 128), dtype=_x0.dtype)
    del _x0
    return _d

def reference(L0_attn_a_x, L0_attn_a_Wi, L0_attn_a_bi, L0_attn_a_Wx, L0_attn_a_bx, L0_attn_a_Wdt, L0_attn_a_bdt, L0_attn_a_A_log, L0_attn_a_Dp, L0_attn_a_Wo, L0_attn_a_bo, L0_attn_a_gamma, L0_attn_a_beta, L0_attn_b_Lambda_re, L0_attn_b_Lambda_im, L0_attn_b_B, L0_attn_b_C, L0_attn_b_D, L0_attn_b_log_step, L0_ffn_Wg, L0_ffn_W1, L0_ffn_W2, L0_ffn_W3):

    def _L0_attn_a_ref(x, Wi, bi, Wx, bx, Wdt, bdt, A_log, Dp, Wo, bo, gamma, beta):
        import jax, jax.numpy as jnp
        import numpy as np
        B, L, D_MODEL = (4, 256, 128)
        D_STATE = 64
        EXPAND = 2
        D_INNER = EXPAND * D_MODEL
        EPS = 1e-05

        def _s6_forward(x, Wi, bi, Wx, bx, Wdt, bdt, A_log, Dp, Wo, bo, gamma, beta):
            residual = x
            x_and_res = x @ Wi + bi
            xs, res = jnp.split(x_and_res, [D_INNER], axis=-1)
            xs = jax.nn.silu(xs)
            x_dbl = xs @ Wx + bx
            d_raw = x_dbl[..., :D_STATE]
            B_sel = x_dbl[..., D_STATE:2 * D_STATE]
            C_sel = x_dbl[..., 2 * D_STATE:]
            delta = jax.nn.softplus(d_raw @ Wdt + bdt)
            A = -jnp.exp(A_log.astype(jnp.float32))

            def step(h, t):
                delta_t, B_t, x_t, C_t = t
                dA = jnp.exp(delta_t[..., None] * A)
                dB = delta_t[..., None] * B_t[:, None, :]
                h = dA * h + dB * x_t[..., None]
                y_t = C_t * jnp.sum(h, axis=-1)
                return (h, y_t)
            seq = (jnp.moveaxis(delta, 1, 0), jnp.moveaxis(B_sel, 1, 0), jnp.moveaxis(xs, 1, 0), jnp.moveaxis(C_sel, 1, 0))
            h0 = jnp.zeros((x.shape[0], D_INNER, D_STATE), x.dtype)
            _, y = jax.lax.scan(step, h0, seq)
            y = jnp.moveaxis(y, 0, 1)
            y = y + xs * Dp
            y = y * jax.nn.silu(res)
            out = y @ Wo + bo
            z = out + residual
            mu = jnp.mean(z, axis=-1, keepdims=True)
            var = jnp.mean((z - mu) ** 2, axis=-1, keepdims=True)
            return gamma * (z - mu) / jnp.sqrt(var + EPS) + beta
        return _s6_forward(x, Wi, bi, Wx, bx, Wdt, bdt, A_log, Dp, Wo, bo, gamma, beta)

    def _L0_attn_b_ref(u, Lambda_re, Lambda_im, B, C, D, log_step):
        import jax, jax.numpy as jnp
        import numpy as np
        DT_MIN, DT_MAX = (0.001, 0.1)
        STEP_RESCALE = 1.0

        def _s5_forward(u, Lambda_re, Lambda_im, B, C, D, log_step):
            Lambda = jnp.minimum(Lambda_re, -0.0001) + 1j * Lambda_im
            B_tilde = (B[..., 0] + 1j * B[..., 1]).astype(jnp.complex64)
            C_tilde = (C[..., 0] + 1j * C[..., 1]).astype(jnp.complex64)
            step = STEP_RESCALE * jnp.exp(log_step[:, 0])
            Lambda_bar = jnp.exp(Lambda * step)
            B_bar = ((Lambda_bar - 1.0) / Lambda)[:, None] * B_tilde
            Bu = jnp.einsum('blh,ph->blp', u.astype(jnp.complex64), B_bar)
            A = jnp.broadcast_to(Lambda_bar, Bu.shape)

            def combine(e_i, e_j):
                a_i, b_i = e_i
                a_j, b_j = e_j
                return (a_j * a_i, a_j * b_i + b_j)
            _, xs = jax.lax.associative_scan(combine, (A, Bu), axis=1)
            ys = jnp.einsum('blp,hp->blh', xs, C_tilde).real + D * u
            return ys
        return _s5_forward(u, Lambda_re, Lambda_im, B, C, D, log_step)

    def _L0_ffn_ref(x, Wg, W1, W2, W3):
        import jax, jax.numpy as jnp
        import numpy as np
        E = 8
        TOP_K = 2
        DIM = 128
        HID = 256
        B, T, C = x.shape
        xf = x.reshape(-1, C)
        logits = xf @ Wg
        top_w, top_i = jax.lax.top_k(logits, TOP_K)
        top_w = jax.nn.softmax(top_w, axis=-1)
        one_hot = jax.nn.one_hot(top_i, E, dtype=xf.dtype)
        combine = jnp.einsum('nk,nke->ne', top_w, one_hot)
        h = jnp.einsum('nc,ech->enh', xf, W1)
        g = jnp.einsum('nc,ech->enh', xf, W2)
        y = jnp.einsum('enh,ehc->enc', jax.nn.silu(h) * g, W3)
        out = jnp.einsum('enc,ne->nc', y, combine)
        return out.reshape(B, T, C)
    x = L0_attn_a_x
    x = x + _L0_attn_a_ref(_layernorm(x, axis=-1), L0_attn_a_Wi, L0_attn_a_bi, L0_attn_a_Wx, L0_attn_a_bx, L0_attn_a_Wdt, L0_attn_a_bdt, L0_attn_a_A_log, L0_attn_a_Dp, L0_attn_a_Wo, L0_attn_a_bo, L0_attn_a_gamma, L0_attn_a_beta)
    x = x + _L0_ffn_ref(_layernorm(x, axis=-1), L0_ffn_Wg, L0_ffn_W1, L0_ffn_W2, L0_ffn_W3)
    x = x + _L0_attn_b_ref(_layernorm(x, axis=-1), L0_attn_b_Lambda_re, L0_attn_b_Lambda_im, L0_attn_b_B, L0_attn_b_C, L0_attn_b_D, L0_attn_b_log_step)
    x = x + _L0_ffn_ref(_layernorm(x, axis=-1), L0_ffn_Wg, L0_ffn_W1, L0_ffn_W2, L0_ffn_W3)
    return x

_drawn_inputs = setup_inputs


def setup_inputs(seed=0):
    import zlib

    import numpy as np

    out = dict(_drawn_inputs(seed))
    spreads = {'L0_attn_a_bi': (0.0, 0.1),
     'L0_attn_a_bx': (0.0, 0.1),
     'L0_attn_a_bdt': (0.0, 0.384),
     'L0_attn_a_bo': (0.0, 0.409),
     'L0_attn_a_gamma': (1.0, 0.2),
     'L0_attn_a_beta': (0.0, 0.1)}
    factors = {'L0_attn_a_Dp': 8.0,
     'L0_ffn_Wg': 8.0,
     'L0_ffn_W1': 8.0,
     'L0_ffn_W2': 8.0,
     'L0_ffn_W3': 8.0}
    for name, (base, spread) in spreads.items():
        noise = np.random.default_rng([zlib.crc32(name.encode()), seed]).standard_normal(out[name].shape)
        drawn = base * np.exp(spread * noise) if base else spread * noise
        out[name] = jnp.asarray(drawn.astype(out[name].dtype))
    for name, factor in factors.items():
        out[name] = (out[name] * factor).astype(out[name].dtype)
    return out
```

```python
from contextlib import ExitStack

import concourse.bass as bass
from concourse import mybir

ALU = mybir.AluOpType
ACT = mybir.ActivationFunctionType
F32 = mybir.dt.float32
BF16 = mybir.dt.bfloat16
I32 = mybir.dt.int32
AX_X = mybir.AxisListType.X

NB, L, D = 8, 512, 128
DI, NS = 256, 64
E, HID = 8, 256
TT = L // 128
PAIRS = DI // 2
HALF = PAIRS // 2
QUADS, PER_QUAD = 4, 16
EPS = 1e-5
LOWEST = -1e30
YLAG = 3
POOL_TURNS = 3
POOLED = PAIRS * POOL_TURNS // 4
PI = 3.141592653589793

MOE_AT = {1: 27, 2: 94}
LN_AT = [17, 7, 12, 62, 79]
ROUTE = 20
LOADS = 39
PE_STEPS = [
    (5, "post", "X", "z"), (17, "post", "X", "x1T"), (19, "post", "X", "lg1"), (25, "post", "X", "cp1"),
    (61, "post", "X", "y1t"), (68, "post", "X", "uT"), (70, "post", "H", "P1"), (70, "post", "G", "P2"),
    (76, "post", "Y", "s5"), (78, "post", "X", "s5t"), (84, "post", "X", "x3T"), (86, "post", "X", "lg2"),
    (92, "post", "X", "cp2"), (128, "post", "X", "y2t"),
    (22, "pre", "H", "xnT"), (23, "pre", "G", "in0"), (24, "pre", "H", "in1"), (25, "pre", "G", "in2"),
    (26, "pre", "H", "in3"), (62, "pre", "H", "draw"), (63, "pre", "G", "Bp"), (64, "pre", "H", "C0"),
    (65, "pre", "G", "C1"), (67, "pre", "H", "dt0"), (68, "pre", "G", "dt1"),
]
for _m, _s in MOE_AT.items():
    PE_STEPS += [(_s + 3, "post", "Y", f"y{_m}")]
    PE_STEPS += [(_s + 4 * _e - 1, "post", "X", f"cb{_m}_{_e}") for _e in range(E)]
    PE_STEPS += [(_s + 2 * _j, "post", "H", f"h{_m}_{_j}") for _j in range(2 * E)]
    PE_STEPS += [(_s + 2 * _j + 1, "post", "G", f"g{_m}_{_j}") for _j in range(2 * E)]
PE_STEPS.sort(key=lambda s: (s[0], s[1] != "post"))
SLOT = {name: slot for slot, _, _, name in PE_STEPS}
BANK = {name: bank for _, _, bank, name in PE_STEPS}


class Turn:

    def __init__(self, b, pre, post, pres, posts):
        self.b, self.pre, self.post, self.pres, self.posts = b, pre, post, pres, posts

    def before(self, name):
        bank = BANK[name]
        steps = [s for s in PE_STEPS if s[2] == bank]
        per = {kind: sum(s[1] == kind for s in steps) for kind in ("pre", "post")}
        here = [s[3] for s in steps if (s[1] == "pre" and self.pre) or (s[1] == "post" and self.post)]
        return 1 + self.pres * per["pre"] + self.posts * per["post"] + here.index(name)


def known(n, below):
    return isinstance(n, int) and n < below


def weave(pair, tasks):
    todo = [[t, next(t, None)] for t in tasks]
    for slot in range(PAIRS if pair else 0):
        pair(slot)
        for t in todo:
            while t[1] is not None and t[1] <= slot:
                t[1] = next(t[0], None)
    while any(t[1] is not None for t in todo):
        t = min((t for t in todo if t[1] is not None), key=lambda t: t[1])
        t[1] = next(t[0], None)


def hybrid_kernel(nc, x, Wi, bi, Wx, bx, Wdt, bdt, A_log, Dp, Wo, bo, gamma, beta, Lre, Lim, SB, SC, SD, log_step,
                  Wg, W1, W2, W3, c_ident, c_sel, c_wsum, c_sel8, c_rev, out):
    with ExitStack() as ctx:
        def sb(name, shape, dt=F32):
            return ctx.enter_context(nc.sbuf_tensor(name, shape, dt))

        def sem(name):
            return ctx.enter_context(nc.semaphore(name))

        wi = sb("wi", [128, 2 * DI]); wx = sb("wx", [128, 2, 2 * NS + DI]); wxb = sb("wxb", [128, 2, 128])
        wdt = sb("wdt", [NS, DI]); wo = sb("wo", [128, 2, D]); wg = sb("wg", [128, E])
        w1 = sb("w1", [128, E, HID]); w2 = sb("w2", [128, E, HID]); w3 = sb("w3", [128, E, 2, D])
        ident = sb("ident", [128, 128]); identb = sb("identb", [128, 128], BF16)
        sel = sb("sel", [96, PER_QUAD, 128], BF16)
        wsum = sb("wsum", [128, PER_QUAD, 32])
        sel8 = sb("sel8", [24, E, 128], BF16)
        rev = sb("rev", [128, E])
        hbi = sb("hbi", [128, 4]); bxd = sb("bxd", [NS, 1]); bxb = sb("bxb", [128, 1]); bxc = sb("bxc", [128, 2])
        bdts = sb("bdts", [128, 2]); dps_ = sb("dps_", [128, 2]); rows = sb("rows", [1, 3, D]); bcs = sb("bcs", [128, 3, D])
        ones1 = sb("ones1", [1, 128]); one_col = sb("one_col", [128, 1]); mhalf = sb("mhalf", [128, TT])
        al = sb("al", [128, 128]); nega = sb("nega", [128, 128])
        s5p = sb("s5p", [128, 3]); s5w = sb("s5w", [128, 32]); s5i = sb("s5i", [128, 1], I32)
        sbt = sb("sbt", [NS, D, 2]); sct = sb("sct", [128, NS, 2]); bb = sb("bb", [NS, 4, D])
        cc = sb("cc", [128, 2, 2, NS]); mb = sb("mb", [128, 2, 128]); mc = sb("mc", [128, 2, 128])
        cosT = sb("cosT", [128, L]); sinT = sb("sinT", [128, L]); rT = sb("rT", [128, L]); sdt = sb("sdt", [128, 1])
        xnew = sb("xnew", [128, TT, D]); xn = sb("xn", [128, TT, D]); xnT = sb("xnT", [128, L])
        th = sb("th", [128, 2, L]); vh = sb("vh", [128, 2, L]); xs = sb("xs", [128, 2, L]); sres = sb("sres", [128, 2, L])
        draw = sb("draw", [NS, L]); btmp = sb("btmp", [128, L]); cm = sb("cm", [128, 2, L])
        spa = sb("spa", [128, 2, L]); du = sb("du", [128, 2, 2, L])
        rest = sb("rest", [128, L]); parts = sb("parts", [128, 2, 3, 2, L], BF16)
        pdu = sb("pdu", [96, 2, 8, L], BF16); bdup = sb("bdup", [128, L])
        cg = sb("cg", [128, 2, L]); xd = sb("xd", [128, 2, L]); resa = sb("resa", [128, TT, D]); resb = sb("resb", [128, TT, D])
        ub = sb("ub", [128, 2, L]); w = sb("w", [128, 4, L]); h = sb("h", [128, 4, L])
        yt = sb("yt", [128, L]); y3 = sb("y3", [128, 2, L])
        z = sb("z", [128, TT, D]); x1 = sb("x1", [128, TT, D]); nrm = sb("nrm", [128, TT, D]); nT = sb("nT", [128, L])
        bst = sb("bst", [128, 5, TT, 6]); bag = sb("bag", [128, 5, TT, 2]); var = sb("var", [128, 5, TT]); rs = sb("rs", [128, 5, TT])
        lg = sb("lg", [128, TT, E]); rt = sb("rt", [128, 8, TT, E]); rc = sb("rc", [128, 8, TT])
        cpb = sb("cpb", [128, TT, 24], BF16); cpT = sb("cpT", [24, L], BF16)
        xc = sb("xc", [128, 2, L]); tq = sb("tq", [128, 2, L]); sq = sb("sq", [128, 2, L]); aq = sb("aq", [128, 2, L])
        yT = sb("yT", [128, L]); zt = sb("zt", [128, 4, L])

        banks = {n: ctx.enter_context(nc.psum_tensor("bank" + n, [128, 512], F32)) for n in "HGXY"}
        dtp = [ctx.enter_context(nc.psum_tensor(f"dtp{j}", [128, 512], F32)) for j in range(2)]
        up = ctx.enter_context(nc.psum_tensor("up", [128, 512], F32))
        ys = ctx.enter_context(nc.psum_tensor("ys", [128, 512], F32))

        filled = {n: sem("filled" + n) for n in "HGXY"}
        drained = {n: sem("drained" + n) for n in "HGXY"}
        loads = sem("loads"); x_in = sem("x_in"); x_out = sem("x_out")
        ones_ready = sem("ones_ready"); angles_ready = sem("angles_ready"); matrices_ready = sem("matrices_ready")
        setup_done = sem("setup_done"); setup_chain = sem("setup_chain"); rows_spread = sem("rows_spread")
        matrices_turned = sem("matrices_turned"); setup_a = sem("setup_a")
        parts_in = [sem("parts_in0"), sem("parts_in1")]; ready = sem("ready")
        d_bc = sem("d_bc"); u_bc = sem("u_bc"); u_taken = sem("u_taken"); da = sem("da"); wq = sem("wq")
        scanned = sem("scanned"); summed = sem("summed"); ys_taken = sem("ys_taken")
        b_ready = sem("b_ready"); gate_ready = sem("gate_ready"); res_ready = sem("res_ready")
        st_s = [sem(f"st_s{k}") for k in range(5)]; ag_s = [sem(f"ag_s{k}") for k in range(5)]; var_s = [sem(f"var_s{k}") for k in range(5)]
        rs_s = [sem(f"rs_s{k}") for k in range(5)]; nrm_s = [sem(f"nrm_s{k}") for k in range(5)]
        th_s = sem("th_s"); silu_s = sem("silu_s"); abs_s = sem("abs_s"); e_s = sem("e_s"); ln_s = sem("ln_s")
        relu_s = sem("relu_s"); du_s = sem("du_s"); hi_s = sem("hi_s"); mid_s = sem("mid_s"); rest_s = sem("rest_s"); lo_s = sem("lo_s")
        yt_s = sem("yt_s"); y3_s = sem("y3_s"); z_s = sem("z_s"); zg_s = sem("zg_s"); x1_s = sem("x1_s")
        gap_s = sem("gap_s"); gap_e = sem("gap_e"); route = sem("route"); cpb_s = sem("cpb_s")
        xc_s = sem("xc_s"); tanh_s = sem("tanh_s"); act_used = sem("act_used")
        zt_s = sem("zt_s"); zb_s = sem("zb_s"); zs_s = sem("zs_s"); q1_s = sem("q1_s"); q2_s = sem("q2_s")
        s5_s = sem("s5_s"); x2_s = sem("x2_s"); x3_s = sem("x3_s"); x4_s = sem("x4_s")

        block = ctx.enter_context(nc.Block())

        def turns(eng, pre_a, scan, post):
            weave(None, [pre_a(Turn(-1, True, False, 0, 0))])
            scan(Turn(0, True, False, 1, 0))
            with eng.Fori(1, NB - 1) as b:
                scan(Turn(b, True, True, b + 1, b - 1))
            scan(Turn(NB - 1, False, True, NB, NB - 2))
            weave(None, [post(Turn(NB, False, True, NB, NB - 1))])

        def tasks_of(t, pre_a, post, extra=()):
            return ([post(t)] if t.post else []) + ([pre_a(t)] if t.pre else []) + list(extra)

        @block.sync
        def _(sp):
            sp.sem_inc(x_out, 16)
            loaded = []

            def load(dst, src):
                loaded.append(sp.dma_start(dst, src).then_inc(loads, 16))

            def load_columns(dst, src, at, n):
                for m in range(n):
                    load(dst[:, m:m + 1], src[at + 128 * m:at + 128 * (m + 1)].rearrange("(p a) -> p a", a=1))

            load(ident[:, :], c_ident)
            load(wi[:, :], Wi)
            load_columns(hbi, bi, 0, 4)
            sp.dma_start(xnew[:, :, :], x[0].rearrange("(a p) c -> p a c", p=128)).then_inc(x_in, 16)
            load(wx[:, :, :], Wx.rearrange("(k p) n -> p k n", p=128))
            load(wdt[:, :], Wdt)
            load(bxd[:, :], bx[0:NS].rearrange("(p a) -> p a", a=1))
            for j in range(2):
                load(bxb[64 * j:64 * j + 64, :], bx[NS:2 * NS].rearrange("(p a) -> p a", a=1))
            load_columns(bxc, bx, 2 * NS, 2)
            load_columns(bdts, bdt, 0, 2)
            load_columns(dps_, Dp, 0, 2)
            load(al[:, :], A_log.rearrange("(d j) n -> d (j n)", j=2))
            load(sel[:, :, :], c_sel.rearrange("k (i m) -> k i m", m=128))
            load(wsum[:, :, :], c_wsum.rearrange("k (i m) -> k i m", m=32))
            for n, v in enumerate((bo, gamma, beta)):
                load(rows[:, n, :], v.rearrange("(a n) -> a n", a=1))
            for j in range(2):
                for n, v in enumerate((Lre.rearrange("(p a) -> p a", a=1), Lim.rearrange("(p a) -> p a", a=1), log_step)):
                    load(s5p[64 * j:64 * j + 64, n:n + 1], v)
            load(sbt[:, :, :], SB)
            load(sct[:, :, :], SC)
            load(sdt[:, :], SD.rearrange("(p a) -> p a", a=1))
            load(wo[:, :, :], Wo.rearrange("(k p) n -> p k n", p=128))
            load(wg[:, :], Wg)
            load(sel8[:, :, :], c_sel8.rearrange("k (i m) -> k i m", m=128))
            load(rev[:, :], c_rev)
            load(w1[:, :, :], W1.rearrange("e c h -> c e h"))
            load(w2[:, :, :], W2.rearrange("e c h -> c e h"))
            load(w3[:, :, :, :], W3.rearrange("e (k p) c -> p e k c", p=128))

            assert len(loaded) == LOADS

            def send_parts(i, half):
                sp.wait_ge(lo_s, 4 * i + 2 * half + 2)
                for s in range(2):
                    for part in range(3):
                        for q in range(QUADS):
                            sp.dma_start(pdu[32 * part:32 * part + 32, s, 4 * half + q, :],
                                         parts[32 * q:32 * q + 32, s, part, half, :]).then_inc(parts_in[half], 16)

            def pre_a(t):
                i = t.b + 1
                if not known(t.b, 0):
                    sp.wait_ge(res_ready, 2 * i)
                    sp.dma_start(xnew[:, :, :], x[i].rearrange("(a p) c -> p a c", p=128)).then_inc(x_in, 16)
                    sp.wait_ge(u_bc, PAIRS * t.b + HALF)
                    sp.wait_ge(d_bc, PAIRS * t.b + HALF)
                send_parts(i, 0)

            def scan(t):
                if not known(t.b, 1):
                    sp.wait_ge(u_bc, PAIRS * t.b)
                    sp.wait_ge(d_bc, PAIRS * t.b)
                send_parts(t.b, 1)
                if t.pre:
                    pre_a(t)
                if t.post:
                    post(t)

            def post(t):
                c = t.b - 1
                sp.wait_ge(x4_s, c + 1)
                sp.dma_start(out[c].rearrange("(a p) c -> p a c", p=128), z[:, :, :]).then_inc(x_out, 16)

            pre_a(Turn(-1, True, False, 0, 0))
            scan(Turn(0, True, False, 1, 0))
            with sp.Fori(1, NB - 1) as b:
                scan(Turn(b, True, True, b + 1, b - 1))
            scan(Turn(NB - 1, False, True, NB, NB - 2))
            post(Turn(NB, False, True, NB, NB - 1))
            sp.wait_ge(x_out, 16 * NB + 16)

        @block.tensor
        def _(pe):
            def claim(t, name):
                pe.wait_ge(drained[BANK[name]], t.before(name))
                return banks[BANK[name]]

            def is_filled(t, name, ins):
                ins.then_inc(filled[BANK[name]], 1)

            def turn_tiles(t, name, src):
                p = claim(t, name)
                for a in range(TT):
                    ins = nc.tensor.transpose(p[:, a * 128:(a + 1) * 128], src(a), ident[:, :])
                is_filled(t, name, ins)

            for n in "HGXY":
                pe.sem_inc(filled[n], 1)
            pe.wait_ge(loads, 16 * LOADS)
            pe.wait_ge(setup_a, 1)
            nc.tensor.transpose(up[:, 0:128], al[:, :], ident[:, :])
            pe.wait_ge(ones_ready, 1)
            nc.tensor.matmul(dtp[0][:, 0:3 * D], ones1[:, :], rows[:, :, :].rearrange("a n c -> a (n c)"),
                             start=True, stop=True).then_inc(rows_spread, 1)
            pe.wait_ge(matrices_ready, 1)
            for j in range(4):
                nc.tensor.transpose(dtp[1][:, j * 64:(j + 1) * 64], bb[:, j, :], ident[0:64, 0:64])
            for j in range(2):
                ins = nc.tensor.transpose(ys[:, j * 128:(j + 1) * 128], cc[:, j, :, :].rearrange("h c p -> h (c p)"), ident[:, :])
            ins.then_inc(matrices_turned, 1)
            pe.wait_ge(setup_done, 1)

            def pre_a(t):
                i = t.b + 1
                yield SLOT["xnT"]
                pe.wait_ge(nrm_s[0], 4 * i + 4)
                turn_tiles(t, "xnT", lambda a: xn[:, a, :])
                for m in range(4):
                    yield SLOT[f"in{m}"]
                    p = claim(t, f"in{m}")
                    if m == 0:
                        pe.wait_ge(drained["H"], t.before("xnT") + 1)
                    is_filled(t, f"in{m}", nc.tensor.matmul(p[:, :], wi[:, m * 128:(m + 1) * 128], xnT[:, :],
                                                            start=True, stop=True))
                for name, lhs in (("draw", lambda k: wx[:, k, 0:NS]), ("Bp", lambda k: wxb[:, k, :]),
                                  ("C0", lambda k: wx[:, k, 2 * NS:2 * NS + 128]),
                                  ("C1", lambda k: wx[:, k, 2 * NS + 128:2 * NS + 256])):
                    yield SLOT[name]
                    p = claim(t, name)
                    if name == "draw":
                        pe.wait_ge(silu_s, 4 * i + 2)
                    o = p[0:NS, :] if name == "draw" else p[:, :]
                    for k in range(2):
                        ins = nc.tensor.matmul(o, lhs(k), xs[:, k, :], start=(k == 0), stop=(k == 1))
                    is_filled(t, name, ins)
                for m in range(2):
                    yield SLOT[f"dt{m}"]
                    p = claim(t, f"dt{m}")
                    if m == 0:
                        pe.wait_ge(drained["H"], t.before("draw") + 1)
                    is_filled(t, f"dt{m}", nc.tensor.matmul(p[:, :], wdt[:, m * 128:(m + 1) * 128], draw[:, :],
                                                            start=True, stop=True))

            def moe(t, m):
                c = t.b - 1
                lnk = {1: 2, 2: 4}[m]
                yield SLOT[f"x{2 * m - 1}T"]
                pe.wait_ge(nrm_s[lnk], 4 * c + 4)
                turn_tiles(t, f"x{2 * m - 1}T", lambda a: nrm[:, a, :])
                yield SLOT[f"lg{m}"]
                p = claim(t, f"lg{m}")
                for a in range(TT):
                    ins = nc.tensor.matmul(p[:, a * E:(a + 1) * E], nT[:, a * 128:(a + 1) * 128], wg[:, :],
                                           start=True, stop=True)
                is_filled(t, f"lg{m}", ins)
                yield SLOT[f"cp{m}"]
                p = claim(t, f"cp{m}")
                pe.wait_ge(cpb_s, 2 * c + m)
                for a in range(TT):
                    ins = nc.tensor.transpose(p[0:24, :].bitcast(BF16)[:, a * 128:(a + 1) * 128], cpb[:, a, :], identb[:, :])
                is_filled(t, f"cp{m}", ins)

                def down(j):
                    if j == 0:
                        claim(t, f"y{m}")
                    pe.wait_ge(drained["G"], t.before(f"g{m}_{j}") + 1)
                    ins = nc.tensor.matmul(banks["Y"][:, :], w3[:, j // 2, j % 2, :], aq[:, j % 2, :],
                                           start=(j == 0), stop=(j == 2 * E - 1), skip_group_check=True)
                    if j == 2 * E - 1:
                        is_filled(t, f"y{m}", ins)
                    else:
                        ins.then_inc(act_used, 1)

                for j in range(2 * E):
                    e, k = j // 2, j % 2
                    if k == 0:
                        yield SLOT[f"cb{m}_{e}"]
                        p = claim(t, f"cb{m}_{e}")
                        is_filled(t, f"cb{m}_{e}", nc.tensor.matmul(p[:, :], sel8[:, e, :], cpT[:, :], start=True, stop=True))
                    yield SLOT[f"h{m}_{j}"]
                    p = claim(t, f"h{m}_{j}")
                    is_filled(t, f"h{m}_{j}", nc.tensor.matmul(p[:, :], w1[:, e, k * 128:(k + 1) * 128], nT[:, :],
                                                               start=True, stop=True))
                    yield SLOT[f"g{m}_{j}"]
                    p = claim(t, f"g{m}_{j}")
                    pe.wait_ge(drained["X"], t.before(f"cb{m}_{e}") + 1)
                    is_filled(t, f"g{m}_{j}", nc.tensor.matmul(p[:, :], w2[:, e, k * 128:(k + 1) * 128], xc[:, e % 2, :],
                                                               start=True, stop=True))
                    if j >= 1:
                        yield SLOT[f"g{m}_{j}"]
                        down(j - 1)
                yield MOE_AT[m] + 4 * E + 1
                down(2 * E - 1)
                yield SLOT[f"y{m}t"]
                pe.wait_ge(drained["Y"], t.before(f"y{m}") + 1)
                turn_tiles(t, f"y{m}t", lambda a: yT[:, a * 128:(a + 1) * 128])

            def post(t):
                c = t.b - 1
                yield SLOT["z"]
                p = claim(t, "z")
                pe.wait_ge(y3_s, 2 * c + 2)
                for a in range(TT):
                    for k in range(2):
                        ins = nc.tensor.matmul(p[:, a * 128:(a + 1) * 128], y3[:, k, a * 128:(a + 1) * 128], wo[:, k, :],
                                               start=(k == 0), stop=(k == 1))
                is_filled(t, "z", ins)
                yield from moe(t, 1)
                yield SLOT["uT"]
                pe.wait_ge(nrm_s[3], 4 * c + 4)
                turn_tiles(t, "uT", lambda a: nrm[:, a, :])
                yield SLOT["P1"]
                for k, name in enumerate(("P1", "P2")):
                    p = claim(t, name)
                    if k == 0:
                        pe.wait_ge(drained["X"], t.before("uT") + 1)
                    is_filled(t, name, nc.tensor.matmul(p[:, :], mb[:, k, :], nT[:, :], start=True, stop=True))
                yield SLOT["s5"]
                p = claim(t, "s5")
                pe.wait_ge(q1_s, c + 1)
                nc.tensor.matmul(p[:, :], mc[:, 0, :], zt[:, 0, :], start=True, stop=False)
                pe.wait_ge(q2_s, c + 1)
                is_filled(t, "s5", nc.tensor.matmul(p[:, :], mc[:, 1, :], zt[:, 1, :], start=False, stop=True))
                yield SLOT["s5t"]
                pe.wait_ge(drained["Y"], t.before("s5") + 1)
                turn_tiles(t, "s5t", lambda a: yT[:, a * 128:(a + 1) * 128])
                yield from moe(t, 2)

            def scan(t):
                K = PAIRS * t.b

                def sum_states(k):
                    i, q = (k % HALF) // 4, k % 4
                    pe.wait_ge(scanned, K + k + 1)
                    if k % HALF == 0 and not known(K + k, 1):
                        pe.wait_ge(ys_taken, 2 * t.b + k // HALF)
                    nc.tensor.matmul(ys[32 * q:32 * q + 32, :], wsum[:, i, :], h[:, k % 4, :],
                                     start=(i == 0), stop=(i == PER_QUAD - 1)).then_inc(summed, 1)

                def pair(k):
                    i, q, half = (k % HALF) // 4, k % 4, k // HALF
                    if k % HALF == 0:
                        pe.wait_ge(parts_in[half], 384 * t.b + 384)
                    if not known(K + k, 2):
                        pe.wait_ge(scanned, K + k - 1)
                    nc.tensor.matmul(dtp[k % 2][:, :], sel[:, i, :], pdu[:, 0, 4 * half + q, :],
                                     start=True, stop=True).then_inc(d_bc, 1)
                    if not known(K + k, 1):
                        pe.wait_ge(u_taken, K + k)
                    nc.tensor.matmul(up[:, :], sel[:, i, :], pdu[:, 1, 4 * half + q, :],
                                     start=True, stop=True).then_inc(u_bc, 1)
                    if k >= YLAG:
                        sum_states(k - YLAG)

                def tail():
                    yield PAIRS
                    for k in range(PAIRS - YLAG, PAIRS):
                        sum_states(k)

                weave(pair, [tail()] + tasks_of(t, pre_a, post))

            turns(pe, pre_a, scan, post)

        @block.scalar
        def _(act):
            A = nc.scalar.activation

            def got(t, name):
                act.wait_ge(filled[BANK[name]], t.before(name) + 1)
                return banks[BANK[name]]

            def copy_out(t, name, dst, src=None, func=ACT.Copy, **kw):
                p = got(t, name)
                A(dst, p[:, :] if src is None else src(p), func, **kw).then_inc(drained[BANK[name]], 1)

            act.wait_ge(loads, 16 * LOADS)
            A(al[:, :], al[:, :], ACT.Exp).then_inc(setup_a, 1)
            A(s5w[:, 0:1], s5p[:, 2:3], ACT.Exp).then_inc(setup_a, 1)
            act.wait_ge(angles_ready, 1)
            A(s5w[:, 3:4], s5w[:, 2:3], ACT.Exp).then_inc(setup_a, 1)
            A(s5w[:, 6:7], s5w[:, 4:5], ACT.Sin).then_inc(setup_a, 1)
            A(s5w[:, 7:8], s5w[:, 5:6], ACT.Sin).then_inc(setup_a, 1)
            act.wait_ge(setup_done, 1)

            def pre_a(t):
                i = t.b + 1
                yield SLOT["xnT"] + 1
                copy_out(t, "xnT", xnT[:, :])
                for m in range(4):
                    yield SLOT[f"in{m}"] + 1
                    p = got(t, f"in{m}")
                    if m >= 2:
                        act.wait_ge(silu_s, 4 * i + m - 1)
                    elif not known(i, 1):
                        act.wait_ge(silu_s, 4 * i)
                    A(th[:, m % 2, :], p[:, :], ACT.Tanh, bias=hbi[:, m:m + 1], scale=0.5).then_inc(th_s, 1)
                    A(vh[:, m % 2, :], p[:, :], ACT.Identity, bias=hbi[:, m:m + 1], scale=0.5)\
                        .then_inc(drained[BANK[f"in{m}"]], 1)
                yield SLOT["draw"] + 1
                copy_out(t, "draw", draw[:, :], lambda p: p[0:NS, :], ACT.Identity, bias=bxd[:, 0:1])
                yield SLOT["Bp"] + 1
                if not known(i, 1):
                    act.wait_ge(b_ready, i)
                    act.wait_ge(gate_ready, 4 * i)
                copy_out(t, "Bp", btmp[:, :], None, ACT.Identity, bias=bxb[:, 0:1])
                for m in range(2):
                    yield SLOT[f"C{m}"] + 1
                    copy_out(t, f"C{m}", cm[:, m, :], None, ACT.Identity, bias=bxc[:, m:m + 1])
                for m in range(2):
                    yield SLOT[f"dt{m}"] + 1
                    p = got(t, f"dt{m}")
                    if m == 0 and not known(i, 1):
                        act.wait_ge(du_s, 4 * i)
                    A(spa[:, m, :], p[:, :], ACT.Abs, bias=bdts[:, m:m + 1]).then_inc(abs_s, 1)
                yield SLOT["dt1"] + 2
                act.wait_ge(abs_s, 2 * i + 2)
                A(spa[:, :, :], spa[:, :, :], ACT.Exp, scale=-1.0).then_inc(e_s, 1)
                yield SLOT["dt1"] + 4
                act.wait_ge(e_s, i + 1)
                A(spa[:, :, :], spa[:, :, :], ACT.Ln, bias=one_col[:, 0:1]).then_inc(ln_s, 1)
                for half in range(2):
                    for s in range(2):
                        r = 4 * i + 2 * half + s
                        yield SLOT["dt1"] + 8 + 6 * half + 3 * s
                        act.wait_ge(du_s, r + 1)
                        if half == 0 and s == 0 and not known(i, 1):
                            act.wait_ge(parts_in[0], 384 * i)
                        if half == 1 and s == 0 and not known(i, 1):
                            act.wait_ge(parts_in[1], 384 * i)
                        A(parts[:, s, 0, half, :], du[:, s, half, :], ACT.Copy).then_inc(hi_s, 1)
                        yield SLOT["dt1"] + 10 + 6 * half + 3 * s
                        act.wait_ge(rest_s, r + 1)
                        A(parts[:, s, 1, half, :], rest[:, :], ACT.Copy).then_inc(mid_s, 1)
                act.wait_ge(drained["G"], t.before("Bp") + 1)

            def moe(t, m):
                c = t.b - 1
                yield SLOT[f"x{2 * m - 1}T"] + 1
                copy_out(t, f"x{2 * m - 1}T", nT[:, :])
                yield SLOT[f"lg{m}"] + 4
                act.wait_ge(gap_s, 2 * c + m)
                A(rc[:, 5, :], rc[:, 4, :], ACT.Exp).then_inc(gap_e, 1)
                yield SLOT[f"cp{m}"] + 1
                copy_out(t, f"cp{m}", cpT[:, :], lambda p: p[0:24, :].bitcast(BF16)[:, 0:L])
                for j in range(2 * E):
                    yield SLOT[f"h{m}_{j}"] + 1
                    p = got(t, f"h{m}_{j}")
                    if j >= 2:
                        act.wait_ge(drained["H"], t.before(f"h{m}_{j - 2}") + 1)
                    A(tq[:, j % 2, :], p[:, :], ACT.Tanh, scale=0.5).then_inc(tanh_s, 1)
                yield SLOT[f"y{m}t"] - 1
                copy_out(t, f"y{m}", yT[:, :])

            def post(t):
                yield from moe(t, 1)
                yield SLOT["uT"] + 1
                copy_out(t, "uT", nT[:, :])
                yield from moe(t, 2)

            def scan(t):
                K = PAIRS * t.b
                N = POOLED * t.b

                def pair(k):
                    half, i, q = k // HALF, (k % HALF) // 4, k % 4
                    col = HALF * half + PER_QUAD * q + i
                    act.wait_ge(d_bc, K + k + 1)
                    A(dtp[k % 2][:, :], dtp[k % 2][:, :], ACT.Exp, scale=nega[:, col:col + 1]).then_inc(da, 1)
                    if k == 0:
                        if not known(K, 1):
                            act.wait_ge(wq, N)
                            act.wait_ge(u_taken, K)
                        A(bdup[:, :], btmp[:, :], ACT.Copy).then_inc(b_ready, 1)
                    if k % 4 < POOL_TURNS:
                        n = (k // 4) * POOL_TURNS + k % 4
                        act.wait_ge(u_bc, K + k + 1)
                        if not known(N + n, 2):
                            act.wait_ge(wq, N + n - 1)
                        A(ub[:, n % 2, :], up[:, :], ACT.Copy).then_inc(u_taken, 1)

                weave(pair, tasks_of(t, pre_a, post))

            turns(act, pre_a, scan, post)

        @block.gpsimd
        def _(pool):
            def rstd(k, i, at):
                yield at
                pool.wait_ge(var_s[k], i + 1)
                nc.gpsimd.tensor_tensor(rs[:, k, :], var[:, k, :], mhalf[:, :], ALU.pow).then_inc(rs_s[k], 1)

            pool.wait_ge(loads, 16 * LOADS)
            pool.wait_ge(setup_done, 1)

            def pre_a(t):
                yield from rstd(0, t.b + 1, LN_AT[0] + 1)

            def post(t):
                for k in range(1, 5):
                    yield from rstd(k, t.b - 1, LN_AT[k] + 1)

            def scan(t):
                K = PAIRS * t.b

                def pair(k):
                    if k % 4 < POOL_TURNS:
                        n = (k // 4) * POOL_TURNS + k % 4
                        if k == 0:
                            pool.wait_ge(b_ready, t.b + 1)
                        pool.wait_ge(u_taken, K + k + 1)
                        if not known(K + k, 4):
                            pool.wait_ge(scanned, K + k - 3)
                        nc.gpsimd.tensor_tensor(w[:, k % 4, :], ub[:, n % 2, :], bdup[:, :], ALU.mult).then_inc(wq, 1)

                weave(pair, tasks_of(t, pre_a, post))

            turns(pool, pre_a, scan, post)

        @block.vector
        def _(v):
            V = nc.vector
            step = [0]

            def got(t, name):
                v.wait_ge(filled[BANK[name]], t.before(name) + 1)
                return banks[BANK[name]]

            def drain(name, ins):
                ins.then_inc(drained[BANK[name]], 1)

            def chain(ins):
                step[0] += 1
                ins.then_inc(setup_chain, 1)
                v.wait_ge(setup_chain, step[0])

            chain(V.memset(one_col[:, :], 1.0))
            chain(V.memset(mhalf[:, :], -0.5))
            chain(V.memset(ones1[:, :], 1.0))
            v.sem_inc(ones_ready, 1)
            v.wait_ge(loads, 16 * LOADS)
            chain(V.tensor_copy(identb[:, :], ident[:, :]))
            chain(V.tensor_scalar(hbi[:, :], hbi[:, :], 0.5, None, ALU.mult))
            for k in range(2):
                for j in range(2):
                    chain(V.tensor_copy(wxb[:, k, 64 * j:64 * j + 64], wx[:, k, NS:2 * NS]))
            S = lambda n: s5w[:, n:n + 1]
            v.wait_ge(setup_a, 2)
            chain(V.tensor_scalar(S(1), s5p[:, 0:1], -1e-4, None, ALU.min))
            chain(V.tensor_tensor(S(2), S(1), S(0), ALU.mult))
            chain(V.tensor_tensor(S(8), s5p[:, 1:2], S(0), ALU.mult))
            chain(V.tensor_scalar(S(9), S(8), 1.0 / (2 * PI), None, ALU.mult))
            chain(V.tensor_copy(s5i[:, :], S(9)))
            chain(V.tensor_copy(S(10), s5i[:, :]))
            chain(V.scalar_tensor_tensor(S(8), S(10), -6.28125, S(8), ALU.mult, ALU.add))
            chain(V.scalar_tensor_tensor(S(8), S(10), -(2 * PI - 6.28125), S(8), ALU.mult, ALU.add))
            chain(V.tensor_scalar(S(4), S(8), 0.5, None, ALU.mult))
            chain(V.tensor_scalar(S(5), S(4), -1.0, None, ALU.mult))
            chain(V.tensor_tensor(S(5), S(4), S(5), ALU.max))
            chain(V.tensor_scalar(S(5), S(5), -1.0, PI / 2, ALU.mult, ALU.add))
            v.wait_ge(rows_spread, 1)
            chain(V.tensor_scalar(nega[:, :], up[:, 0:128], -1.0, None, ALU.mult))
            chain(V.tensor_copy(bcs[:, :, :].rearrange("p n c -> p (n c)"), dtp[0][:, 0:3 * D]))
            v.sem_inc(angles_ready, 1)
            v.wait_ge(setup_a, 5)
            c_, s_, er = S(11), S(12), S(3)
            chain(V.tensor_tensor(S(13), S(6), S(6), ALU.mult))
            chain(V.tensor_scalar(S(13), S(13), 2.0, None, ALU.mult))
            chain(V.tensor_scalar(c_, S(13), -1.0, 1.0, ALU.mult, ALU.add))
            chain(V.tensor_tensor(s_, S(6), S(7), ALU.mult))
            chain(V.tensor_scalar(s_, s_, 2.0, None, ALU.mult))
            chain(V.tensor_scalar(S(14), er, -1.0, None, ALU.add))
            chain(V.tensor_tensor(S(15), er, S(13), ALU.mult))
            chain(V.tensor_tensor(S(14), S(14), S(15), ALU.subtract))
            chain(V.tensor_tensor(S(15), er, s_, ALU.mult))
            chain(V.tensor_tensor(S(16), S(1), S(1), ALU.mult))
            chain(V.scalar_tensor_tensor(S(16), s5p[:, 1:2], s5p[:, 1:2], S(16), ALU.mult, ALU.add))
            chain(V.reciprocal(S(16), S(16)))
            chain(V.tensor_tensor(S(17), S(15), s5p[:, 1:2], ALU.mult))
            chain(V.scalar_tensor_tensor(S(17), S(14), S(1), S(17), ALU.mult, ALU.add))
            chain(V.tensor_tensor(S(17), S(17), S(16), ALU.mult))
            chain(V.tensor_tensor(S(18), S(14), s5p[:, 1:2], ALU.mult))
            chain(V.scalar_tensor_tensor(S(18), S(15), S(1), S(18), ALU.mult, ALU.subtract))
            chain(V.tensor_tensor(S(18), S(18), S(16), ALU.mult))
            fr, fi = s5w[0:NS, 17:18], s5w[0:NS, 18:19]
            chain(V.tensor_scalar(bb[:, 3, :], sbt[:, :, 1], fi, None, ALU.mult))
            chain(V.scalar_tensor_tensor(bb[:, 0, :], sbt[:, :, 0], fr, bb[:, 3, :], ALU.mult, ALU.subtract))
            chain(V.tensor_scalar(bb[:, 3, :], sbt[:, :, 0], fi, None, ALU.mult))
            chain(V.scalar_tensor_tensor(bb[:, 1, :], sbt[:, :, 1], fr, bb[:, 3, :], ALU.mult, ALU.add))
            chain(V.tensor_copy(bb[:, 2, :], bb[:, 1, :]))
            chain(V.tensor_scalar(bb[:, 3, :], bb[:, 0, :], -1.0, None, ALU.mult))
            chain(V.tensor_copy(cc[:, 0, 0, :], sct[:, :, 0]))
            chain(V.tensor_scalar(cc[:, 0, 1, :], sct[:, :, 1], -1.0, None, ALU.mult))
            chain(V.tensor_copy(cc[:, 1, 0, :], cc[:, 0, 1, :]))
            chain(V.tensor_scalar(cc[:, 1, 1, :], sct[:, :, 0], -1.0, None, ALU.mult))
            v.sem_inc(matrices_ready, 1)
            chain(V.memset(cosT[:, 0:1], 1.0))
            chain(V.memset(sinT[:, 0:1], 0.0))
            n = 1
            while n < L:
                chain(V.tensor_scalar(rT[:, 0:n], sinT[:, 0:n], s_, None, ALU.mult))
                chain(V.scalar_tensor_tensor(cosT[:, n:2 * n], cosT[:, 0:n], c_, rT[:, 0:n], ALU.mult, ALU.subtract))
                chain(V.tensor_scalar(rT[:, 0:n], cosT[:, 0:n], s_, None, ALU.mult))
                chain(V.scalar_tensor_tensor(sinT[:, n:2 * n], sinT[:, 0:n], c_, rT[:, 0:n], ALU.mult, ALU.add))
                chain(V.tensor_tensor(S(19), s_, s_, ALU.mult))
                chain(V.tensor_tensor(S(20), c_, s_, ALU.mult))
                chain(V.tensor_tensor(S(21), c_, c_, ALU.mult))
                chain(V.tensor_tensor(c_, S(21), S(19), ALU.subtract))
                chain(V.tensor_scalar(s_, S(20), 2.0, None, ALU.mult))
                n *= 2
            chain(V.tensor_scalar(rT[:, :], cosT[:, :], 0.0, er, ALU.mult, ALU.add))
            v.wait_ge(matrices_turned, 1)
            chain(V.tensor_copy(mb[:, :, :].rearrange("p n c -> p (n c)"), dtp[1][:, 0:256]))
            chain(V.tensor_copy(mc[:, :, :].rearrange("p n c -> p (n c)"), ys[:, 0:256]))
            for n in "HGXY":
                v.sem_inc(drained[n], 1)
            v.sem_inc(setup_done, 1)

            def layer_norm(k, i, at, src, dst):
                yield at
                for a in range(TT):
                    ins = V.bn_stats(bst[:, k, a, :], src[:, a, :]).then_inc(st_s[k], 1)
                v.wait_ge(st_s[k], 4 * i + 4)
                v.nop(nofuse=True)
                for a in range(TT):
                    ins = V.bn_aggr(bag[:, k, a, :], bst[:, k, a, :]).then_inc(ag_s[k], 1)
                v.wait_ge(ag_s[k], 4 * i + 4)
                V.tensor_scalar(var[:, k, :], bag[:, k, :, 1], EPS, None, ALU.add).then_inc(var_s[k], 1)
                yield at + 3
                v.wait_ge(rs_s[k], i + 1)
                for a in range(TT):
                    V.tensor_scalar(dst[:, a, :], src[:, a, :], bag[:, k, a, 0:1], rs[:, k, a:a + 1],
                                    ALU.subtract, ALU.mult).then_inc(nrm_s[k], 1)

            def pre_a(t):
                i = t.b + 1
                yield LN_AT[0]
                v.wait_ge(x_in, 16 * i + 16)
                if not known(i, 1):
                    v.wait_ge(res_ready, 2 * i)
                yield from layer_norm(0, i, LN_AT[0], xnew, xn)
                for m in range(4):
                    yield SLOT[f"in{m}"] + 2
                    v.wait_ge(th_s, 4 * i + m + 1)
                    v.wait_ge(drained[BANK[f"in{m}"]], t.before(f"in{m}") + 1)
                    dst = xs[:, m, :] if m < 2 else sres[:, m - 2, :]
                    V.scalar_tensor_tensor(dst, th[:, m % 2, :], 1.0, vh[:, m % 2, :], ALU.add, ALU.mult).then_inc(silu_s, 1)
                for m in range(2):
                    yield SLOT[f"dt{m}"] + 2
                    p = got(t, f"dt{m}")
                    v.wait_ge(abs_s, 2 * i + m + 1)
                    if m == 0 and not known(i, 1):
                        v.wait_ge(lo_s, 4 * i)
                    drain(f"dt{m}", V.tensor_scalar(du[:, 0, m, :], p[:, :], bdts[:, m:m + 1], 0.0, ALU.add, ALU.max))
                for half in range(2):
                    for s in range(2):
                        r = 4 * i + 2 * half + s
                        yield SLOT["dt1"] + 7 + 6 * half + 3 * s
                        if s == 0:
                            v.wait_ge(ln_s, i + 1)
                            v.wait_ge(drained[BANK[f"dt{half}"]], t.before(f"dt{half}") + 1)
                            V.tensor_tensor(du[:, 0, half, :], du[:, 0, half, :], spa[:, half, :], ALU.add).then_inc(du_s, 1)
                        else:
                            v.wait_ge(du_s, r)
                            v.wait_ge(silu_s, 4 * i + half + 1)
                            V.tensor_tensor(du[:, 1, half, :], du[:, 0, half, :], xs[:, half, :], ALU.mult).then_inc(du_s, 1)
                        yield SLOT["dt1"] + 9 + 6 * half + 3 * s
                        v.wait_ge(hi_s, r + 1)
                        if not known(r, 1):
                            v.wait_ge(lo_s, r)
                        V.tensor_tensor(rest[:, :], du[:, s, half, :], parts[:, s, 0, half, :], ALU.subtract).then_inc(rest_s, 1)
                        yield SLOT["dt1"] + 11 + 6 * half + 3 * s
                        v.wait_ge(mid_s, r + 1)
                        V.tensor_tensor(parts[:, s, 2, half, :], rest[:, :], parts[:, s, 1, half, :], ALU.subtract).then_inc(lo_s, 1)
                for m in range(2):
                    v.wait_ge(drained[BANK[f"C{m}"]], t.before(f"C{m}") + 1)

            def take_sums(b, half, t, at):
                yield at
                v.wait_ge(summed, PAIRS * b + HALF * (half + 1))
                v.wait_ge(gate_ready, 4 * b + 4)
                if not known(2 * b + half, 1):
                    v.wait_ge(y3_s, 2 * b + half)
                V.tensor_tensor(yt[:, :], ys[:, :], cg[:, half, :], ALU.mult).then_inc(ys_taken, 1)
                yield at + 1
                v.wait_ge(ys_taken, 2 * b + half + 1)
                if half == 0 and t.post:
                    v.wait_ge(filled["X"], t.before("z") + 1)
                V.tensor_tensor(y3[:, half, :], yt[:, :], xd[:, half, :], ALU.add).then_inc(y3_s, 1)

            def pre_b(t):
                b = t.b
                yield 6
                if not known(b, 1):
                    v.wait_ge(y3_s, 2 * b)
                v.wait_ge(silu_s, 4 * b + 4)
                for half in range(2):
                    V.tensor_tensor(cg[:, half, :], cm[:, half, :], sres[:, half, :], ALU.mult).then_inc(gate_ready, 1)
                    V.scalar_tensor_tensor(xd[:, half, :], xs[:, half, :], dps_[:, half:half + 1], sres[:, half, :],
                                           ALU.mult, ALU.mult).then_inc(gate_ready, 1)
                yield 12
                if t.post:
                    v.wait_ge(x1_s, b)
                v.wait_ge(nrm_s[0], 4 * b + 4)
                V.tensor_tensor(resa[:, :, :], xn[:, :, :], bcs[:, 0:1, :].to_broadcast([128, TT, D]), ALU.add).then_inc(res_ready, 1)
                V.tensor_tensor(resb[:, :, :], xnew[:, :, :], bcs[:, 2:3, :].to_broadcast([128, TT, D]), ALU.add).then_inc(res_ready, 1)

            def moe(t, m):
                c = t.b - 1
                yield SLOT[f"lg{m}"] + 1
                p = got(t, f"lg{m}")
                drain(f"lg{m}", V.tensor_copy(lg[:, :, :].rearrange("p a e -> p (a e)"), p[:, 0:TT * E]))
                v.wait_ge(drained["X"], t.before(f"lg{m}") + 1)
                done = [0]
                r0 = ROUTE * (2 * c + m - 1)

                def link(ins):
                    done[0] += 1
                    ins.then_inc(route, 1)
                    v.wait_ge(route, r0 + done[0])

                R = lambda n: rt[:, n, :, :]
                def bc(n):
                    return rc[:, n, :].unsqueeze(2).to_broadcast([128, TT, E])
                revb = rev[:, :].unsqueeze(1).to_broadcast([128, TT, E])
                src = lg[:, :, :]
                for n in range(2):
                    link(V.tensor_reduce(rc[:, n, :], src, AX_X, ALU.max))
                    link(V.tensor_tensor(R(0), src, bc(n), ALU.is_equal))
                    link(V.tensor_tensor(R(0), R(0), revb, ALU.mult))
                    link(V.tensor_reduce(rc[:, 2 + n, :], R(0), AX_X, ALU.max))
                    link(V.tensor_tensor(R(1 + n), R(0), bc(2 + n), ALU.is_equal))
                    if n == 0:
                        link(V.scalar_tensor_tensor(R(3), R(1), LOWEST, lg[:, :, :], ALU.mult, ALU.add))
                        src = R(3)
                        yield SLOT[f"lg{m}"] + 2
                V.tensor_tensor(rc[:, 4, :], rc[:, 1, :], rc[:, 0, :], ALU.subtract).then_inc(gap_s, 1)
                yield SLOT[f"lg{m}"] + 5
                v.wait_ge(gap_e, 2 * c + m)
                link(V.tensor_scalar(rc[:, 6, :], rc[:, 5, :], 1.0, 2.0, ALU.add, ALU.mult))
                link(V.reciprocal(rc[:, 6, :], rc[:, 6, :]))
                link(V.tensor_tensor(rc[:, 7, :], rc[:, 6, :], rc[:, 5, :], ALU.mult))
                link(V.tensor_tensor(R(4), R(1), bc(6), ALU.mult))
                link(V.tensor_tensor(R(5), R(2), bc(7), ALU.mult))
                link(V.tensor_tensor(R(4), R(4), R(5), ALU.add))
                link(V.tensor_copy(cpb[:, :, 0:8], R(4)))
                link(V.tensor_tensor(R(4), R(4), cpb[:, :, 0:8], ALU.subtract))
                link(V.tensor_copy(cpb[:, :, 8:16], R(4)))
                V.tensor_tensor(cpb[:, :, 16:24], R(4), cpb[:, :, 8:16], ALU.subtract).then_inc(cpb_s, 1)
                assert done[0] == ROUTE
                a0 = 2 * (2 * E - 1) * c + (2 * E - 1) * (m - 1)

                def gate(j):
                    p = got(t, f"g{m}_{j}")
                    v.wait_ge(drained["H"], t.before(f"h{m}_{j}") + 1)
                    if j >= 2:
                        v.wait_ge(act_used, a0 + j - 1)
                    drain(f"g{m}_{j}", V.tensor_tensor(aq[:, j % 2, :], sq[:, j % 2, :], p[:, :], ALU.mult))

                for j in range(2 * E):
                    e = j // 2
                    if j % 2 == 0:
                        yield SLOT[f"cb{m}_{e}"] + 1
                        p = got(t, f"cb{m}_{e}")
                        if e >= 2:
                            v.wait_ge(filled["G"], t.before(f"g{m}_{2 * e - 3}") + 1)
                        drain(f"cb{m}_{e}", V.tensor_tensor(xc[:, e % 2, :], p[:, :], nT[:, :], ALU.mult))
                    yield SLOT[f"h{m}_{j}"] + 1
                    p = got(t, f"h{m}_{j}")
                    v.wait_ge(tanh_s, 4 * E * c + 2 * E * (m - 1) + j + 1)
                    drain(f"h{m}_{j}", V.scalar_tensor_tensor(sq[:, j % 2, :], tq[:, j % 2, :], 1.0, p[:, :],
                                                              ALU.add, ALU.mult))
                    yield SLOT[f"g{m}_{j}"] + 1
                    gate(j)
                yield SLOT[f"y{m}t"] + 1
                got(t, f"y{m}t")

            def post(t):
                c = t.b - 1
                yield from take_sums(c, 1, t, 2)
                yield SLOT["z"] + 2
                p = got(t, "z")
                v.wait_ge(res_ready, 2 * c + 2)
                v.wait_ge(x_out, 16 * c + 16)
                drain("z", V.tensor_tensor(z[:, :, :].rearrange("p a c -> p (a c)"), p[:, :],
                                           resa[:, :, :].rearrange("p a c -> p (a c)"), ALU.add))
                v.wait_ge(drained["X"], t.before("z") + 1)
                yield from layer_norm(1, c, LN_AT[1], z, nrm)
                yield LN_AT[1] + 4
                v.wait_ge(nrm_s[1], 4 * c + 4)
                V.tensor_tensor(nrm[:, :, :], nrm[:, :, :], bcs[:, 1:2, :].to_broadcast([128, TT, D]), ALU.mult).then_inc(zg_s, 1)
                yield LN_AT[1] + 4
                v.wait_ge(zg_s, c + 1)
                V.tensor_tensor(x1[:, :, :], nrm[:, :, :], resb[:, :, :], ALU.add).then_inc(x1_s, 1)
                v.wait_ge(x1_s, c + 1)
                yield from layer_norm(2, c, LN_AT[2], x1, nrm)
                yield from moe(t, 1)
                flat = lambda ap: ap[:, :, :].rearrange("p a c -> p (a c)")
                p = banks["X"]
                drain("y1t", V.tensor_tensor(flat(x1), flat(x1), p[:, :], ALU.add))
                v.wait_ge(drained["X"], t.before("y1t") + 1)
                yield from layer_norm(3, c, LN_AT[3], x1, nrm)
                yield SLOT["P1"] + 1
                p1, p2 = got(t, "P1"), got(t, "P2")
                drain("P1", V.tensor_tensor(zt[:, 2, :], p1[:, :], cosT[:, :], ALU.mult))
                drain("P2", V.tensor_tensor(zt[:, 3, :], p2[:, :], sinT[:, :], ALU.mult))
                yield SLOT["P1"] + 2
                v.wait_ge(drained["H"], t.before("P1") + 1)
                v.wait_ge(drained["G"], t.before("P2") + 1)
                V.tensor_tensor(zt[:, 2, :], zt[:, 2, :], zt[:, 3, :], ALU.add).then_inc(zb_s, 1)
                yield SLOT["P1"] + 3
                v.wait_ge(zb_s, c + 1)
                V.tensor_tensor_scan(zt[:, 3, :], rT[:, :], zt[:, 2, :], 0.0, ALU.mult, ALU.add).then_inc(zs_s, 1)
                yield SLOT["P1"] + 4
                v.wait_ge(zs_s, c + 1)
                V.tensor_tensor(zt[:, 0, :], zt[:, 3, :], cosT[:, :], ALU.mult).then_inc(q1_s, 1)
                yield SLOT["P1"] + 5
                V.tensor_tensor(zt[:, 1, :], zt[:, 3, :], sinT[:, :], ALU.mult).then_inc(q2_s, 1)
                yield SLOT["s5"] + 1
                p = got(t, "s5")
                drain("s5", V.scalar_tensor_tensor(yT[:, :], nT[:, :], sdt[:, 0:1], p[:, :], ALU.mult, ALU.add))
                yield SLOT["s5t"] + 1
                p = got(t, "s5t")
                drain("s5t", V.tensor_tensor(flat(x1), flat(x1), p[:, :], ALU.add))
                v.wait_ge(drained["X"], t.before("s5t") + 1)
                yield from layer_norm(4, c, LN_AT[4], x1, nrm)
                yield from moe(t, 2)
                drain("y2t", V.tensor_tensor(flat(z), flat(x1), banks["X"][:, :], ALU.add))
                v.wait_ge(drained["X"], t.before("y2t") + 1)
                v.sem_inc(x4_s, 1)

            def scan(t):
                K = PAIRS * t.b
                N = POOLED * t.b

                def pair(k):
                    if k % 4 >= POOL_TURNS:
                        if k == POOL_TURNS:
                            v.wait_ge(b_ready, t.b + 1)
                        v.wait_ge(u_bc, K + k + 1)
                        V.tensor_tensor(w[:, k % 4, :], up[:, :], bdup[:, :], ALU.mult).then_inc(u_taken, 1)
                    v.wait_ge(da, K + k + 1)
                    if k % 4 < POOL_TURNS:
                        v.wait_ge(wq, N + (k // 4) * POOL_TURNS + k % 4 + 1)
                    else:
                        v.wait_ge(u_taken, K + k + 1)
                    if not known(K + k, 4):
                        v.wait_ge(summed, K + k - 3)
                    V.tensor_tensor_scan(h[:, k % 4, :], dtp[k % 2][:, :], w[:, k % 4, :], 0.0,
                                         ALU.mult, ALU.add).then_inc(scanned, 1)

                weave(pair, [pre_b(t), take_sums(t.b, 0, t, HALF + 2)] + tasks_of(t, pre_a, post))

            turns(v, pre_a, scan, post)


_INS = ['L0_attn_a_x', 'L0_attn_a_Wi', 'L0_attn_a_bi', 'L0_attn_a_Wx', 'L0_attn_a_bx', 'L0_attn_a_Wdt', 'L0_attn_a_bdt',
        'L0_attn_a_A_log', 'L0_attn_a_Dp', 'L0_attn_a_Wo', 'L0_attn_a_bo', 'L0_attn_a_gamma', 'L0_attn_a_beta',
        'L0_attn_b_Lambda_re', 'L0_attn_b_Lambda_im', 'L0_attn_b_B', 'L0_attn_b_C', 'L0_attn_b_D', 'L0_attn_b_log_step',
        'L0_ffn_Wg', 'L0_ffn_W1', 'L0_ffn_W2', 'L0_ffn_W3']


def kernel(**inputs):
    import ml_dtypes
    import numpy as _np
    import concourse.bacc as _bacc
    from concourse import mybir as _mybir
    from concourse.bass_utils import run_bass_kernel_spmd as _run

    i, r, col = _np.arange(16)[None, :, None], _np.arange(96)[:, None, None] % 32, _np.arange(128)[None, None, :]
    sel = (r == 2 * i + col // 64).astype(ml_dtypes.bfloat16).reshape(96, 16 * 128)
    p, c32 = _np.arange(128)[:, None, None], _np.arange(32)[None, None, :]
    wsum = (c32 == 2 * i + p // 64).astype(_np.float32).reshape(128, 16 * 32)
    e = _np.arange(24)[:, None, None] % 8
    sel8 = _np.broadcast_to(e == _np.arange(8)[None, :, None], (24, 8, 128)).astype(ml_dtypes.bfloat16).reshape(24, 8 * 128)
    rev = _np.broadcast_to(8.0 - _np.arange(8), (128, 8)).astype(_np.float32)
    constants = {"c_ident": _np.eye(128, dtype=_np.float32), "c_sel": sel, "c_wsum": wsum, "c_sel8": sel8, "c_rev": rev}

    nc = _bacc.Bacc("TRN2", target_bir_lowering=False, num_devices=1)
    arrays, args = {}, []
    for name, a in [(n, inputs[n]) for n in _INS] + list(constants.items()):
        a = _np.ascontiguousarray(a)
        arrays[f"in_{name}_dram"] = a
        args.append(nc.dram_tensor(f"in_{name}_dram", a.shape, _mybir.dt.from_np(a.dtype), kind="ExternalInput").ap())
    args.append(nc.dram_tensor("out_0_dram", (8, 512, 128), _mybir.dt.float32, kind="ExternalOutput").ap())
    hybrid_kernel(nc, *args)
    r = _run(nc, [arrays], core_ids=[0])
    return r.results[0]["out_0_dram"]
```

```python
from contextlib import ExitStack

import concourse.bass as bass
from concourse import mybir

ALU = mybir.AluOpType
ACT = mybir.ActivationFunctionType
F32 = mybir.dt.float32
BF16 = mybir.dt.bfloat16
I32 = mybir.dt.int32
AX_X = mybir.AxisListType.X

NB, L, D = 8, 512, 128
DI, NS = 256, 64
E, HID = 8, 256
TT = L // 128
PAIRS = DI // 2
HALF = PAIRS // 2
QUADS, PER_QUAD = 4, 16
EPS = 1e-5
LOWEST = -1e30
D_RING, U_RING, UB_RING, W_RING, H_RING = 2, 1, 2, 4, 8
SUM_AT = 6
U_LEAD = 1
Y_LAG = 3
ADD_LAG = 1
PI = 3.141592653589793

MOE_AT = {1: 19, 2: 81}
TILE_SLOTS = 2
LN_AT = [50, 7, 11, 55, 74]
ROUTE = 17
LOADS = 38
PE_STEPS = [
    (5, "post", "Y", "z"), (16, "post", "Y", "x1T"), (19, "post", "Y", "lg1"),
    (60, "post", "Y", "uT"), (63, "post", "H", "P1"), (63, "post", "G", "P2"),
    (70, "post", "H", "s5"), (73, "post", "Y", "s5t"), (79, "post", "Y", "x3T"), (81, "post", "Y", "lg2"),
    (56, "pre", "H", "xnT"), (58, "pre", "G", "in0"), (59, "pre", "X", "in1"), (60, "pre", "H", "in2"),
    (61, "pre", "G", "in3"), (65, "pre", "X", "draw"), (66, "pre", "H", "Bp"), (67, "pre", "G", "C0"),
    (68, "pre", "X", "C1"), (72, "pre", "G", "dt0"), (73, "pre", "X", "dt1"),
]
for _m, _s in MOE_AT.items():
    PE_STEPS += [(_s + TILE_SLOTS * _j, "post", "HGX"[2 * _j % 3], f"h{_m}_{_j}") for _j in range(2 * E)]
    PE_STEPS += [(_s + TILE_SLOTS * _j + 1, "post", "HGX"[(2 * _j + 1) % 3], f"g{_m}_{_j}") for _j in range(2 * E)]
    PE_STEPS += [(_s + TILE_SLOTS * (2 * _e + 1) + 1 + Y_LAG, "post", "Y", f"y{_m}_{_e}") for _e in range(E)]
PE_STEPS.sort(key=lambda s: (s[0], s[1] != "post"))
SLOT = {name: slot for slot, _, _, name in PE_STEPS}
BANK = {name: bank for _, _, bank, name in PE_STEPS}


def last_user(k, ring):
    return k - ring if k >= ring else max(j for j in range(PAIRS) if j % ring == k % ring) - PAIRS


MOE_PE = sorted([(0, "lg", 0)] + [(TILE_SLOTS * j, "h", j) for j in range(2 * E)]
                + [(TILE_SLOTS * j + 1, "g", j) for j in range(2 * E)]
                + [(TILE_SLOTS * (2 * e + 1) + 1 + Y_LAG, "y", e) for e in range(E)], key=lambda s: s[0])


class Turn:

    def __init__(self, b, pre, post, pres, posts):
        self.b, self.pre, self.post, self.pres, self.posts = b, pre, post, pres, posts

    def before(self, name):
        bank = BANK[name]
        steps = [s for s in PE_STEPS if s[2] == bank]
        per = {kind: sum(s[1] == kind for s in steps) for kind in ("pre", "post")}
        here = [s[3] for s in steps if (s[1] == "pre" and self.pre) or (s[1] == "post" and self.post)]
        return 1 + self.pres * per["pre"] + self.posts * per["post"] + here.index(name)


MOE_V = sorted([(TILE_SLOTS * j + 1, "h", j) for j in range(2 * E)] + [(TILE_SLOTS * j + 2, "g", j) for j in range(2 * E)]
               + [(TILE_SLOTS * (2 * e + 1) + 2 + Y_LAG + ADD_LAG, "y", e) for e in range(E)], key=lambda s: s[0])


def both(one, other):
    left = [[next(g), g] for g in (one, other)]
    while left:
        first = min(left, key=lambda n: n[0])
        yield first[0]
        first[0] = next(first[1], None)
        left = [n for n in left if n[0] is not None]


def known(n, below):
    return isinstance(n, int) and n < below


def weave(pair, tasks):
    todo = [[t, next(t, None)] for t in tasks]
    for slot in range(PAIRS if pair else 0):
        pair(slot)
        for t in todo:
            while t[1] is not None and t[1] <= slot:
                t[1] = next(t[0], None)
    while any(t[1] is not None for t in todo):
        t = min((t for t in todo if t[1] is not None), key=lambda t: t[1])
        t[1] = next(t[0], None)


def hybrid_kernel(nc, x, Wi, bi, Wx, bx, Wdt, bdt, A_log, Dp, Wo, bo, gamma, beta, Lre, Lim, SB, SC, SD, log_step,
                  Wg, W1, W2, W3, c_ident, c_sel, c_wsum, c_rev, out):
    with ExitStack() as ctx:
        def sb(name, shape, dt=F32):
            return ctx.enter_context(nc.sbuf_tensor(name, shape, dt))

        def sem(name):
            return ctx.enter_context(nc.semaphore(name))

        wi = sb("wi", [128, 2 * DI]); wx = sb("wx", [128, 2, 2 * NS + DI]); wxb = sb("wxb", [128, 2, 128])
        wdt = sb("wdt", [NS, DI]); wo = sb("wo", [128, 2, D]); wg = sb("wg", [128, E])
        w1 = sb("w1", [128, E, HID]); w2 = sb("w2", [128, E, HID]); w3 = sb("w3", [128, E, 2, D])
        ident = sb("ident", [128, 128])
        sel = sb("sel", [96, PER_QUAD, 128], BF16)
        wsum = sb("wsum", [128, PER_QUAD, 32])
        rev = sb("rev", [128, E])
        hbi = sb("hbi", [128, 4]); bxd = sb("bxd", [NS, 1]); bxb = sb("bxb", [128, 1]); bxc = sb("bxc", [128, 2])
        bdts = sb("bdts", [128, 2]); dps_ = sb("dps_", [128, 2]); rows = sb("rows", [1, 3, D]); bcs = sb("bcs", [128, 3, D])
        ones1 = sb("ones1", [1, 128]); one_col = sb("one_col", [128, 1]); mhalf = sb("mhalf", [128, TT])
        al = sb("al", [128, 128]); nega = sb("nega", [128, 128])
        s5p = sb("s5p", [128, 3]); s5w = sb("s5w", [128, 32]); s5i = sb("s5i", [128, 1], I32)
        sbt = sb("sbt", [NS, D, 2]); sct = sb("sct", [128, NS, 2]); bb = sb("bb", [NS, 4, D])
        cc = sb("cc", [128, 2, 2, NS]); mb = sb("mb", [128, 2, 128]); mc = sb("mc", [128, 2, 128])
        cosT = sb("cosT", [128, L]); sinT = sb("sinT", [128, L]); rT = sb("rT", [128, L]); sdt = sb("sdt", [128, 1])
        xnew = sb("xnew", [128, TT, D]); xn = sb("xn", [128, TT, D]); xnT = sb("xnT", [128, L])
        th = sb("th", [128, 2, L]); vh = sb("vh", [128, 2, L]); xs = sb("xs", [128, 2, L]); sres = sb("sres", [128, 2, L])
        draw = sb("draw", [NS, L]); btmp = sb("btmp", [128, L]); cm = sb("cm", [128, 2, L])
        spa = sb("spa", [128, 2, L]); du = sb("du", [128, 2, 2, L])
        rest = sb("rest", [128, L]); parts = sb("parts", [128, 2, 3, 2, L], BF16)
        pdu = sb("pdu", [96, 2, 8, L], BF16); bdup = sb("bdup", [128, L])
        cg = sb("cg", [128, 2, L]); xd = sb("xd", [128, 2, L]); resa = sb("resa", [128, TT, D]); resb = sb("resb", [128, TT, D])
        ub = sb("ub", [128, UB_RING, L]); w = sb("w", [128, W_RING, L]); h = sb("h", [128, H_RING, L])
        yt = sb("yt", [128, L]); y3 = sb("y3", [128, 2, L])
        z = sb("z", [128, TT, D]); x1 = sb("x1", [128, TT, D]); nrm = sb("nrm", [128, TT, D]); nT = sb("nT", [128, L])
        bst = sb("bst", [128, 5, TT, 6]); bag = sb("bag", [128, 5, TT, 2]); var = sb("var", [128, 5, TT]); rs = sb("rs", [128, 5, TT])
        lg = sb("lg", [128, TT, E]); rt = sb("rt", [128, 8, TT, E]); rc = sb("rc", [128, 8, TT])
        tq = sb("tq", [128, 2, L]); sq = sb("sq", [128, 2, L]); aq = sb("aq", [128, 4, L])
        yT = sb("yT", [128, L])
        zt = [tq[:, 0, :], tq[:, 1, :], sq[:, 0, :], sq[:, 1, :]]

        banks = {n: ctx.enter_context(nc.psum_tensor("bank" + n, [128, 512], F32)) for n in "HGXY"}
        dtp = [ctx.enter_context(nc.psum_tensor(f"dtp{j}", [128, 512], F32)) for j in range(D_RING)]
        up = [ctx.enter_context(nc.psum_tensor(f"up{j}", [128, 512], F32)) for j in range(U_RING)]
        ys = ctx.enter_context(nc.psum_tensor("ys", [128, 512], F32))

        filled = {n: sem("filled" + n) for n in "HGXY"}
        drained = {n: sem("drained" + n) for n in "HGXY"}
        loads = sem("loads"); x_in = sem("x_in"); x_out = sem("x_out")
        ones_ready = sem("ones_ready"); angles_ready = sem("angles_ready"); matrices_ready = sem("matrices_ready")
        setup_done = sem("setup_done"); setup_chain = sem("setup_chain"); rows_spread = sem("rows_spread")
        matrices_turned = sem("matrices_turned"); setup_a = sem("setup_a")
        parts_in = [sem("parts_in0"), sem("parts_in1")]; ready = sem("ready")
        d_bc = sem("d_bc"); u_bc = sem("u_bc"); u_copied = sem("u_copied"); da = sem("da"); wq = sem("wq")
        scanned = sem("scanned"); summed = sem("summed"); ys_taken = sem("ys_taken")
        b_ready = sem("b_ready"); gate_ready = sem("gate_ready"); res_ready = sem("res_ready")
        st_s = [sem(f"st_s{k}") for k in range(5)]; ag_s = [sem(f"ag_s{k}") for k in range(5)]; var_s = [sem(f"var_s{k}") for k in range(5)]
        rs_s = [sem(f"rs_s{k}") for k in range(5)]; nrm_s = [sem(f"nrm_s{k}") for k in range(5)]
        th_s = sem("th_s"); silu_s = sem("silu_s"); abs_s = sem("abs_s"); e_s = sem("e_s"); ln_s = sem("ln_s")
        relu_s = sem("relu_s"); du_s = sem("du_s"); hi_s = sem("hi_s"); mid_s = sem("mid_s"); rest_s = sem("rest_s"); lo_s = sem("lo_s")
        yt_s = sem("yt_s"); y3_s = sem("y3_s"); z_s = sem("z_s"); zg_s = sem("zg_s"); x1_s = sem("x1_s")
        gap_s = sem("gap_s"); gap_e = sem("gap_e"); route = sem("route")
        tanh_s = sem("tanh_s"); added = sem("added")
        zt_s = sem("zt_s"); zb_s = sem("zb_s"); zs_s = sem("zs_s"); q1_s = sem("q1_s"); q2_s = sem("q2_s")
        s5_s = sem("s5_s"); x2_s = sem("x2_s"); x3_s = sem("x3_s"); x4_s = sem("x4_s")

        block = ctx.enter_context(nc.Block())

        def turns(eng, pre_a, scan, post):
            weave(None, [pre_a(Turn(-1, True, False, 0, 0))])
            scan(Turn(0, True, False, 1, 0))
            with eng.Fori(1, NB - 1) as b:
                scan(Turn(b, True, True, b + 1, b - 1))
            scan(Turn(NB - 1, False, True, NB, NB - 2))
            weave(None, [post(Turn(NB, False, True, NB, NB - 1))])

        def tasks_of(t, pre_a, post, extra=()):
            return ([post(t)] if t.post else []) + ([pre_a(t)] if t.pre else []) + list(extra)

        @block.sync
        def _(sp):
            sp.sem_inc(x_out, 16)
            loaded = []

            def load(dst, src):
                loaded.append(sp.dma_start(dst, src).then_inc(loads, 16))

            def load_columns(dst, src, at, n):
                for m in range(n):
                    load(dst[:, m:m + 1], src[at + 128 * m:at + 128 * (m + 1)].rearrange("(p a) -> p a", a=1))

            load(ident[:, :], c_ident)
            load(wi[:, :], Wi)
            load_columns(hbi, bi, 0, 4)
            sp.dma_start(xnew[:, :, :], x[0].rearrange("(a p) c -> p a c", p=128)).then_inc(x_in, 16)
            load(wx[:, :, :], Wx.rearrange("(k p) n -> p k n", p=128))
            load(wdt[:, :], Wdt)
            load(bxd[:, :], bx[0:NS].rearrange("(p a) -> p a", a=1))
            for j in range(2):
                load(bxb[64 * j:64 * j + 64, :], bx[NS:2 * NS].rearrange("(p a) -> p a", a=1))
            load_columns(bxc, bx, 2 * NS, 2)
            load_columns(bdts, bdt, 0, 2)
            load_columns(dps_, Dp, 0, 2)
            load(al[:, :], A_log.rearrange("(d j) n -> d (j n)", j=2))
            load(sel[:, :, :], c_sel.rearrange("k (i m) -> k i m", m=128))
            load(wsum[:, :, :], c_wsum.rearrange("k (i m) -> k i m", m=32))
            for n, v in enumerate((bo, gamma, beta)):
                load(rows[:, n, :], v.rearrange("(a n) -> a n", a=1))
            for j in range(2):
                for n, v in enumerate((Lre.rearrange("(p a) -> p a", a=1), Lim.rearrange("(p a) -> p a", a=1), log_step)):
                    load(s5p[64 * j:64 * j + 64, n:n + 1], v)
            load(sbt[:, :, :], SB)
            load(sct[:, :, :], SC)
            load(sdt[:, :], SD.rearrange("(p a) -> p a", a=1))
            load(wo[:, :, :], Wo.rearrange("(k p) n -> p k n", p=128))
            load(wg[:, :], Wg)
            load(rev[:, :], c_rev)
            load(w1[:, :, :], W1.rearrange("e c h -> c e h"))
            load(w2[:, :, :], W2.rearrange("e c h -> c e h"))
            load(w3[:, :, :, :], W3.rearrange("e (k p) c -> p e k c", p=128))

            assert len(loaded) == LOADS

            def send_parts(i, half):
                sp.wait_ge(lo_s, 4 * i + 2 * half + 2)
                for s in range(2):
                    for part in range(3):
                        for q in range(QUADS):
                            sp.dma_start(pdu[32 * part:32 * part + 32, s, 4 * half + q, :],
                                         parts[32 * q:32 * q + 32, s, part, half, :]).then_inc(parts_in[half], 16)

            def pre_a(t):
                i = t.b + 1
                if not known(t.b, 0):
                    sp.wait_ge(res_ready, 2 * i)
                    sp.dma_start(xnew[:, :, :], x[i].rearrange("(a p) c -> p a c", p=128)).then_inc(x_in, 16)
                    sp.wait_ge(u_bc, PAIRS * t.b + HALF)
                    sp.wait_ge(d_bc, PAIRS * t.b + HALF)
                send_parts(i, 0)

            def scan(t):
                if not known(t.b, 1):
                    sp.wait_ge(u_bc, PAIRS * t.b)
                    sp.wait_ge(d_bc, PAIRS * t.b)
                send_parts(t.b, 1)
                if t.pre:
                    pre_a(t)
                if t.post:
                    post(t)

            def post(t):
                c = t.b - 1
                sp.wait_ge(x4_s, c + 1)
                sp.dma_start(out[c].rearrange("(a p) c -> p a c", p=128), x1[:, :, :]).then_inc(x_out, 16)

            pre_a(Turn(-1, True, False, 0, 0))
            scan(Turn(0, True, False, 1, 0))
            with sp.Fori(1, NB - 1) as b:
                scan(Turn(b, True, True, b + 1, b - 1))
            scan(Turn(NB - 1, False, True, NB, NB - 2))
            post(Turn(NB, False, True, NB, NB - 1))
            sp.wait_ge(x_out, 16 * NB + 16)

        @block.tensor
        def _(pe):
            def claim(t, name):
                pe.wait_ge(drained[BANK[name]], t.before(name))
                return banks[BANK[name]]

            def is_filled(t, name, ins):
                ins.then_inc(filled[BANK[name]], 1)

            def turn_tiles(t, name, src):
                p = claim(t, name)
                for a in range(TT):
                    ins = nc.tensor.transpose(p[:, a * 128:(a + 1) * 128], src(a), ident[:, :])
                is_filled(t, name, ins)

            for n in "HGXY":
                pe.sem_inc(filled[n], 1)
            pe.wait_ge(loads, 16 * LOADS)
            pe.wait_ge(setup_a, 1)
            nc.tensor.transpose(up[0][:, 0:128], al[:, :], ident[:, :])
            pe.wait_ge(ones_ready, 1)
            nc.tensor.matmul(dtp[0][:, 0:3 * D], ones1[:, :], rows[:, :, :].rearrange("a n c -> a (n c)"),
                             start=True, stop=True).then_inc(rows_spread, 1)
            pe.wait_ge(matrices_ready, 1)
            for j in range(4):
                nc.tensor.transpose(dtp[1][:, j * 64:(j + 1) * 64], bb[:, j, :], ident[0:64, 0:64])
            for j in range(2):
                ins = nc.tensor.transpose(ys[:, j * 128:(j + 1) * 128], cc[:, j, :, :].rearrange("h c p -> h (c p)"), ident[:, :])
            ins.then_inc(matrices_turned, 1)
            pe.wait_ge(setup_done, 1)

            def pre_a(t):
                i = t.b + 1
                yield SLOT["xnT"]
                pe.wait_ge(nrm_s[0], 4 * i + 4)
                turn_tiles(t, "xnT", lambda a: xn[:, a, :])
                for m in range(4):
                    yield SLOT[f"in{m}"]
                    p = claim(t, f"in{m}")
                    if m == 0:
                        pe.wait_ge(drained[BANK["xnT"]], t.before("xnT") + 1)
                    is_filled(t, f"in{m}", nc.tensor.matmul(p[:, :], wi[:, m * 128:(m + 1) * 128], xnT[:, :],
                                                            start=True, stop=True))
                for name, lhs in (("draw", lambda k: wx[:, k, 0:NS]), ("Bp", lambda k: wxb[:, k, :]),
                                  ("C0", lambda k: wx[:, k, 2 * NS:2 * NS + 128]),
                                  ("C1", lambda k: wx[:, k, 2 * NS + 128:2 * NS + 256])):
                    yield SLOT[name]
                    p = claim(t, name)
                    if name == "draw":
                        pe.wait_ge(silu_s, 4 * i + 2)
                    o = p[0:NS, :] if name == "draw" else p[:, :]
                    for k in range(2):
                        ins = nc.tensor.matmul(o, lhs(k), xs[:, k, :], start=(k == 0), stop=(k == 1))
                    is_filled(t, name, ins)
                for m in range(2):
                    yield SLOT[f"dt{m}"]
                    p = claim(t, f"dt{m}")
                    if m == 0:
                        pe.wait_ge(drained[BANK["draw"]], t.before("draw") + 1)
                    is_filled(t, f"dt{m}", nc.tensor.matmul(p[:, :], wdt[:, m * 128:(m + 1) * 128], draw[:, :],
                                                            start=True, stop=True))

            def moe(t, m):
                c = t.b - 1
                lnk = {1: 2, 2: 4}[m]
                yield SLOT[f"x{2 * m - 1}T"]
                pe.wait_ge(nrm_s[lnk], 4 * c + 4)
                turn_tiles(t, f"x{2 * m - 1}T", lambda a: nrm[:, a, :])
                for slot, name, n in MOE_PE:
                    yield MOE_AT[m] + slot
                    if name == "lg":
                        p = claim(t, f"lg{m}")
                        for a in range(TT):
                            ins = nc.tensor.matmul(p[:, a * E:(a + 1) * E], nT[:, a * 128:(a + 1) * 128], wg[:, :],
                                                   start=True, stop=True)
                        is_filled(t, f"lg{m}", ins)
                    elif name in "hg":
                        p, wt = claim(t, f"{name}{m}_{n}"), w1 if name == "h" else w2
                        is_filled(t, f"{name}{m}_{n}", nc.tensor.matmul(p[:, :], wt[:, n // 2, n % 2 * 128:n % 2 * 128 + 128],
                                                                        nT[:, :], start=True, stop=True))
                    else:
                        p = claim(t, f"y{m}_{n}")
                        for k in range(2):
                            pe.wait_ge(drained[BANK[f"g{m}_{2 * n + k}"]], t.before(f"g{m}_{2 * n + k}") + 1)
                        for a in range(TT):
                            for k in range(2):
                                ins = nc.tensor.matmul(p[:, a * 128:(a + 1) * 128], aq[:, (2 * n + k) % 4, a * 128:(a + 1) * 128],
                                                       w3[:, n, k, :], start=(k == 0), stop=(k == 1))
                        is_filled(t, f"y{m}_{n}", ins)

            def post(t):
                c = t.b - 1
                yield SLOT["z"]
                p = claim(t, "z")
                pe.wait_ge(y3_s, 2 * c + 2)
                for a in range(TT):
                    for k in range(2):
                        ins = nc.tensor.matmul(p[:, a * 128:(a + 1) * 128], y3[:, k, a * 128:(a + 1) * 128], wo[:, k, :],
                                               start=(k == 0), stop=(k == 1))
                is_filled(t, "z", ins)
                yield from moe(t, 1)
                yield SLOT["uT"]
                pe.wait_ge(nrm_s[3], 4 * c + 4)
                turn_tiles(t, "uT", lambda a: nrm[:, a, :])
                yield SLOT["P1"]
                for k, name in enumerate(("P1", "P2")):
                    p = claim(t, name)
                    if k == 0:
                        pe.wait_ge(drained[BANK["uT"]], t.before("uT") + 1)
                    is_filled(t, name, nc.tensor.matmul(p[:, :], mb[:, k, :], nT[:, :], start=True, stop=True))
                yield SLOT["s5"]
                p = claim(t, "s5")
                pe.wait_ge(q1_s, c + 1)
                nc.tensor.matmul(p[:, :], mc[:, 0, :], zt[0], start=True, stop=False)
                pe.wait_ge(q2_s, c + 1)
                is_filled(t, "s5", nc.tensor.matmul(p[:, :], mc[:, 1, :], zt[1], start=False, stop=True))
                yield SLOT["s5t"]
                pe.wait_ge(drained[BANK["s5"]], t.before("s5") + 1)
                turn_tiles(t, "s5t", lambda a: yT[:, a * 128:(a + 1) * 128])
                yield from moe(t, 2)

            def scan(t):
                K = PAIRS * t.b

                def sum_states(group):
                    i, half = group % PER_QUAD, group // PER_QUAD
                    pe.wait_ge(scanned, K + 4 * group + 4)
                    if i == 0 and not known(K + group, 1):
                        pe.wait_ge(ys_taken, 2 * t.b + half)
                    for q in range(QUADS):
                        ins = nc.tensor.matmul(ys[32 * q:32 * q + 32, :], wsum[:, i, :], h[:, (4 * group + q) % H_RING, :],
                                               start=(i == 0), stop=(i == PER_QUAD - 1))
                    ins.then_inc(summed, 1)

                def input_(k):
                    i, q, half = (k % HALF) // 4, k % 4, k // HALF
                    if k % HALF == 0:
                        pe.wait_ge(parts_in[half], 384 * t.b + 384)
                    last = last_user(k, U_RING)
                    if not known(K + last, 0):
                        pe.wait_ge(u_copied, K + last + 1)
                    nc.tensor.matmul(up[k % U_RING][:, :], sel[:, i, :], pdu[:, 1, 4 * half + q, :],
                                     start=True, stop=True).then_inc(u_bc, 1)

                def pair(k):
                    i, q, half = (k % HALF) // 4, k % 4, k // HALF
                    if k == 0:
                        for n in range(U_LEAD):
                            input_(n)
                    last = last_user(k, D_RING)
                    if not known(K + last, 0):
                        pe.wait_ge(scanned, K + last + 1)
                    nc.tensor.matmul(dtp[k % D_RING][:, :], sel[:, i, :], pdu[:, 0, 4 * half + q, :],
                                     start=True, stop=True).then_inc(d_bc, 1)
                    if k + U_LEAD < PAIRS:
                        input_(k + U_LEAD)
                    if k % 4 == SUM_AT % 4 and k >= SUM_AT:
                        sum_states((k - SUM_AT) // 4)

                def tail():
                    yield PAIRS
                    for group in range((PAIRS - 1 - SUM_AT) // 4 + 1, PAIRS // 4):
                        sum_states(group)

                weave(pair, [tail()] + tasks_of(t, pre_a, post))

            turns(pe, pre_a, scan, post)

        @block.scalar
        def _(act):
            A = nc.scalar.activation

            def got(t, name):
                act.wait_ge(filled[BANK[name]], t.before(name) + 1)
                return banks[BANK[name]]

            def copy_out(t, name, dst, src=None, func=ACT.Copy, **kw):
                p = got(t, name)
                A(dst, p[:, :] if src is None else src(p), func, **kw).then_inc(drained[BANK[name]], 1)

            act.wait_ge(loads, 16 * LOADS)
            A(al[:, :], al[:, :], ACT.Exp).then_inc(setup_a, 1)
            A(s5w[:, 0:1], s5p[:, 2:3], ACT.Exp).then_inc(setup_a, 1)
            act.wait_ge(angles_ready, 1)
            A(s5w[:, 3:4], s5w[:, 2:3], ACT.Exp).then_inc(setup_a, 1)
            A(s5w[:, 6:7], s5w[:, 4:5], ACT.Sin).then_inc(setup_a, 1)
            A(s5w[:, 7:8], s5w[:, 5:6], ACT.Sin).then_inc(setup_a, 1)
            act.wait_ge(setup_done, 1)

            def pre_a(t):
                i = t.b + 1
                yield SLOT["xnT"] + 1
                copy_out(t, "xnT", xnT[:, :])
                for m in range(4):
                    yield SLOT[f"in{m}"] + 1
                    p = got(t, f"in{m}")
                    if m >= 2:
                        act.wait_ge(silu_s, 4 * i + m - 1)
                    elif not known(i, 1):
                        act.wait_ge(silu_s, 4 * i)
                    A(th[:, m % 2, :], p[:, :], ACT.Tanh, bias=hbi[:, m:m + 1], scale=0.5).then_inc(th_s, 1)
                    A(vh[:, m % 2, :], p[:, :], ACT.Identity, bias=hbi[:, m:m + 1], scale=0.5)\
                        .then_inc(drained[BANK[f"in{m}"]], 1)
                yield SLOT["draw"] + 1
                copy_out(t, "draw", draw[:, :], lambda p: p[0:NS, :], ACT.Identity, bias=bxd[:, 0:1])
                yield SLOT["Bp"] + 1
                if not known(i, 1):
                    act.wait_ge(b_ready, i)
                    act.wait_ge(gate_ready, 4 * i)
                copy_out(t, "Bp", btmp[:, :], None, ACT.Identity, bias=bxb[:, 0:1])
                for m in range(2):
                    yield SLOT[f"C{m}"] + 1
                    copy_out(t, f"C{m}", cm[:, m, :], None, ACT.Identity, bias=bxc[:, m:m + 1])
                for m in range(2):
                    yield SLOT[f"dt{m}"] + 1
                    p = got(t, f"dt{m}")
                    if m == 0 and not known(i, 1):
                        act.wait_ge(du_s, 4 * i)
                    A(spa[:, m, :], p[:, :], ACT.Abs, bias=bdts[:, m:m + 1]).then_inc(abs_s, 1)
                yield SLOT["dt1"] + 2
                act.wait_ge(abs_s, 2 * i + 2)
                A(spa[:, :, :], spa[:, :, :], ACT.Exp, scale=-1.0).then_inc(e_s, 1)
                yield SLOT["dt1"] + 4
                act.wait_ge(e_s, i + 1)
                A(spa[:, :, :], spa[:, :, :], ACT.Ln, bias=one_col[:, 0:1]).then_inc(ln_s, 1)
                for half in range(2):
                    for s in range(2):
                        r = 4 * i + 2 * half + s
                        yield SLOT["dt1"] + 8 + 6 * half + 3 * s
                        act.wait_ge(du_s, r + 1)
                        if half == 0 and s == 0 and not known(i, 1):
                            act.wait_ge(parts_in[0], 384 * i)
                        if half == 1 and s == 0 and not known(i, 1):
                            act.wait_ge(parts_in[1], 384 * i)
                        A(parts[:, s, 0, half, :], du[:, s, half, :], ACT.Copy).then_inc(hi_s, 1)
                        yield SLOT["dt1"] + 10 + 6 * half + 3 * s
                        act.wait_ge(rest_s, r + 1)
                        A(parts[:, s, 1, half, :], rest[:, :], ACT.Copy).then_inc(mid_s, 1)
                act.wait_ge(drained[BANK["Bp"]], t.before("Bp") + 1)

            def moe(t, m):
                c = t.b - 1
                yield SLOT[f"x{2 * m - 1}T"] + 1
                copy_out(t, f"x{2 * m - 1}T", nT[:, :])
                for j in range(2 * E):
                    yield SLOT[f"h{m}_{j}"] + 1
                    p = got(t, f"h{m}_{j}")
                    if j >= 2:
                        act.wait_ge(drained[BANK[f"h{m}_{j - 2}"]], t.before(f"h{m}_{j - 2}") + 1)
                    A(tq[:, j % 2, :], p[:, :], ACT.Tanh, scale=0.5).then_inc(tanh_s, 1)
                    if j == 2:
                        act.wait_ge(gap_s, 2 * c + m)
                        A(rc[:, 5, :], rc[:, 4, :], ACT.Exp).then_inc(gap_e, 1)

            def post(t):
                yield from moe(t, 1)
                yield SLOT["uT"] + 1
                copy_out(t, "uT", nT[:, :])
                yield from moe(t, 2)

            def scan(t):
                K = PAIRS * t.b

                def input_(k):
                    act.wait_ge(u_bc, K + k + 1)
                    if not known(K + k, UB_RING):
                        act.wait_ge(wq, K + k - UB_RING + 1)
                    A(ub[:, k % UB_RING, :], up[k % U_RING][:, :], ACT.Copy).then_inc(u_copied, 1)

                def pair(k):
                    half, i, q = k // HALF, (k % HALF) // 4, k % 4
                    col = HALF * half + PER_QUAD * q + i
                    if k == 0:
                        if not known(K, 1):
                            act.wait_ge(wq, K)
                        A(bdup[:, :], btmp[:, :], ACT.Copy).then_inc(b_ready, 1)
                        for n in range(U_LEAD):
                            input_(n)
                    act.wait_ge(d_bc, K + k + 1)
                    A(dtp[k % D_RING][:, :], dtp[k % D_RING][:, :], ACT.Exp, scale=nega[:, col:col + 1]).then_inc(da, 1)
                    if k + U_LEAD < PAIRS:
                        input_(k + U_LEAD)

                weave(pair, tasks_of(t, pre_a, post))

            turns(act, pre_a, scan, post)

        @block.gpsimd
        def _(pool):
            def rstd(k, i, at):
                yield at
                pool.wait_ge(var_s[k], i + 1)
                nc.gpsimd.tensor_tensor(rs[:, k, :], var[:, k, :], mhalf[:, :], ALU.pow).then_inc(rs_s[k], 1)

            pool.wait_ge(loads, 16 * LOADS)
            pool.wait_ge(setup_done, 1)

            def pre_a(t):
                yield from rstd(0, t.b + 1, LN_AT[0] + 1)

            def post(t):
                for k in range(1, 5):
                    yield from rstd(k, t.b - 1, LN_AT[k] + 1)

            def scan(t):
                K = PAIRS * t.b

                def pair(k):
                    if k == 0:
                        pool.wait_ge(b_ready, t.b + 1)
                    pool.wait_ge(u_copied, K + k + 1)
                    if not known(K + k, W_RING):
                        pool.wait_ge(scanned, K + k - W_RING + 1)
                    nc.gpsimd.tensor_tensor(w[:, k % W_RING, :], ub[:, k % UB_RING, :], bdup[:, :], ALU.mult).then_inc(wq, 1)

                weave(pair, tasks_of(t, pre_a, post))

            turns(pool, pre_a, scan, post)

        @block.vector
        def _(v):
            V = nc.vector
            step = [0]

            def got(t, name):
                v.wait_ge(filled[BANK[name]], t.before(name) + 1)
                return banks[BANK[name]]

            def drain(name, ins):
                ins.then_inc(drained[BANK[name]], 1)

            def chain(ins):
                step[0] += 1
                ins.then_inc(setup_chain, 1)
                v.wait_ge(setup_chain, step[0])

            chain(V.memset(one_col[:, :], 1.0))
            chain(V.memset(mhalf[:, :], -0.5))
            chain(V.memset(ones1[:, :], 1.0))
            v.sem_inc(ones_ready, 1)
            v.wait_ge(loads, 16 * LOADS)
            chain(V.tensor_scalar(hbi[:, :], hbi[:, :], 0.5, None, ALU.mult))
            for k in range(2):
                for j in range(2):
                    chain(V.tensor_copy(wxb[:, k, 64 * j:64 * j + 64], wx[:, k, NS:2 * NS]))
            S = lambda n: s5w[:, n:n + 1]
            v.wait_ge(setup_a, 2)
            chain(V.tensor_scalar(S(1), s5p[:, 0:1], -1e-4, None, ALU.min))
            chain(V.tensor_tensor(S(2), S(1), S(0), ALU.mult))
            chain(V.tensor_tensor(S(8), s5p[:, 1:2], S(0), ALU.mult))
            chain(V.tensor_scalar(S(9), S(8), 1.0 / (2 * PI), None, ALU.mult))
            chain(V.tensor_copy(s5i[:, :], S(9)))
            chain(V.tensor_copy(S(10), s5i[:, :]))
            chain(V.scalar_tensor_tensor(S(8), S(10), -6.28125, S(8), ALU.mult, ALU.add))
            chain(V.scalar_tensor_tensor(S(8), S(10), -(2 * PI - 6.28125), S(8), ALU.mult, ALU.add))
            chain(V.tensor_scalar(S(4), S(8), 0.5, None, ALU.mult))
            chain(V.tensor_scalar(S(5), S(4), -1.0, None, ALU.mult))
            chain(V.tensor_tensor(S(5), S(4), S(5), ALU.max))
            chain(V.tensor_scalar(S(5), S(5), -1.0, PI / 2, ALU.mult, ALU.add))
            v.wait_ge(rows_spread, 1)
            chain(V.tensor_scalar(nega[:, :], up[0][:, 0:128], -1.0, None, ALU.mult))
            chain(V.tensor_copy(bcs[:, :, :].rearrange("p n c -> p (n c)"), dtp[0][:, 0:3 * D]))
            v.sem_inc(angles_ready, 1)
            v.wait_ge(setup_a, 5)
            c_, s_, er = S(11), S(12), S(3)
            chain(V.tensor_tensor(S(13), S(6), S(6), ALU.mult))
            chain(V.tensor_scalar(S(13), S(13), 2.0, None, ALU.mult))
            chain(V.tensor_scalar(c_, S(13), -1.0, 1.0, ALU.mult, ALU.add))
            chain(V.tensor_tensor(s_, S(6), S(7), ALU.mult))
            chain(V.tensor_scalar(s_, s_, 2.0, None, ALU.mult))
            chain(V.tensor_scalar(S(14), er, -1.0, None, ALU.add))
            chain(V.tensor_tensor(S(15), er, S(13), ALU.mult))
            chain(V.tensor_tensor(S(14), S(14), S(15), ALU.subtract))
            chain(V.tensor_tensor(S(15), er, s_, ALU.mult))
            chain(V.tensor_tensor(S(16), S(1), S(1), ALU.mult))
            chain(V.scalar_tensor_tensor(S(16), s5p[:, 1:2], s5p[:, 1:2], S(16), ALU.mult, ALU.add))
            chain(V.reciprocal(S(16), S(16)))
            chain(V.tensor_tensor(S(17), S(15), s5p[:, 1:2], ALU.mult))
            chain(V.scalar_tensor_tensor(S(17), S(14), S(1), S(17), ALU.mult, ALU.add))
            chain(V.tensor_tensor(S(17), S(17), S(16), ALU.mult))
            chain(V.tensor_tensor(S(18), S(14), s5p[:, 1:2], ALU.mult))
            chain(V.scalar_tensor_tensor(S(18), S(15), S(1), S(18), ALU.mult, ALU.subtract))
            chain(V.tensor_tensor(S(18), S(18), S(16), ALU.mult))
            fr, fi = s5w[0:NS, 17:18], s5w[0:NS, 18:19]
            chain(V.tensor_scalar(bb[:, 3, :], sbt[:, :, 1], fi, None, ALU.mult))
            chain(V.scalar_tensor_tensor(bb[:, 0, :], sbt[:, :, 0], fr, bb[:, 3, :], ALU.mult, ALU.subtract))
            chain(V.tensor_scalar(bb[:, 3, :], sbt[:, :, 0], fi, None, ALU.mult))
            chain(V.scalar_tensor_tensor(bb[:, 1, :], sbt[:, :, 1], fr, bb[:, 3, :], ALU.mult, ALU.add))
            chain(V.tensor_copy(bb[:, 2, :], bb[:, 1, :]))
            chain(V.tensor_scalar(bb[:, 3, :], bb[:, 0, :], -1.0, None, ALU.mult))
            chain(V.tensor_copy(cc[:, 0, 0, :], sct[:, :, 0]))
            chain(V.tensor_scalar(cc[:, 0, 1, :], sct[:, :, 1], -1.0, None, ALU.mult))
            chain(V.tensor_copy(cc[:, 1, 0, :], cc[:, 0, 1, :]))
            chain(V.tensor_scalar(cc[:, 1, 1, :], sct[:, :, 0], -1.0, None, ALU.mult))
            v.sem_inc(matrices_ready, 1)
            chain(V.memset(cosT[:, 0:1], 1.0))
            chain(V.memset(sinT[:, 0:1], 0.0))
            n = 1
            while n < L:
                chain(V.tensor_scalar(rT[:, 0:n], sinT[:, 0:n], s_, None, ALU.mult))
                chain(V.scalar_tensor_tensor(cosT[:, n:2 * n], cosT[:, 0:n], c_, rT[:, 0:n], ALU.mult, ALU.subtract))
                chain(V.tensor_scalar(rT[:, 0:n], cosT[:, 0:n], s_, None, ALU.mult))
                chain(V.scalar_tensor_tensor(sinT[:, n:2 * n], sinT[:, 0:n], c_, rT[:, 0:n], ALU.mult, ALU.add))
                chain(V.tensor_tensor(S(19), s_, s_, ALU.mult))
                chain(V.tensor_tensor(S(20), c_, s_, ALU.mult))
                chain(V.tensor_tensor(S(21), c_, c_, ALU.mult))
                chain(V.tensor_tensor(c_, S(21), S(19), ALU.subtract))
                chain(V.tensor_scalar(s_, S(20), 2.0, None, ALU.mult))
                n *= 2
            chain(V.tensor_scalar(rT[:, :], cosT[:, :], 0.0, er, ALU.mult, ALU.add))
            v.wait_ge(matrices_turned, 1)
            chain(V.tensor_copy(mb[:, :, :].rearrange("p n c -> p (n c)"), dtp[1][:, 0:256]))
            chain(V.tensor_copy(mc[:, :, :].rearrange("p n c -> p (n c)"), ys[:, 0:256]))
            for n in "HGXY":
                v.sem_inc(drained[n], 1)
            v.sem_inc(setup_done, 1)

            def layer_norm(k, i, at, src, dst):
                yield at
                for a in range(TT):
                    ins = V.bn_stats(bst[:, k, a, :], src[:, a, :]).then_inc(st_s[k], 1)
                v.wait_ge(st_s[k], 4 * i + 4)
                v.nop(nofuse=True)
                for a in range(TT):
                    ins = V.bn_aggr(bag[:, k, a, :], bst[:, k, a, :]).then_inc(ag_s[k], 1)
                v.wait_ge(ag_s[k], 4 * i + 4)
                V.tensor_scalar(var[:, k, :], bag[:, k, :, 1], EPS, None, ALU.add).then_inc(var_s[k], 1)
                yield at + 3
                v.wait_ge(rs_s[k], i + 1)
                for a in range(TT):
                    V.tensor_scalar(dst[:, a, :], src[:, a, :], bag[:, k, a, 0:1], rs[:, k, a:a + 1],
                                    ALU.subtract, ALU.mult).then_inc(nrm_s[k], 1)

            def pre_a(t):
                i = t.b + 1
                yield LN_AT[0]
                v.wait_ge(x_in, 16 * i + 16)
                if not known(i, 1):
                    v.wait_ge(res_ready, 2 * i)
                yield from layer_norm(0, i, LN_AT[0], xnew, xn)
                for m in range(4):
                    yield SLOT[f"in{m}"] + 2
                    v.wait_ge(th_s, 4 * i + m + 1)
                    v.wait_ge(drained[BANK[f"in{m}"]], t.before(f"in{m}") + 1)
                    dst = xs[:, m, :] if m < 2 else sres[:, m - 2, :]
                    V.scalar_tensor_tensor(dst, th[:, m % 2, :], 1.0, vh[:, m % 2, :], ALU.add, ALU.mult).then_inc(silu_s, 1)
                for m in range(2):
                    yield SLOT[f"dt{m}"] + 2
                    p = got(t, f"dt{m}")
                    v.wait_ge(abs_s, 2 * i + m + 1)
                    if m == 0 and not known(i, 1):
                        v.wait_ge(lo_s, 4 * i)
                    drain(f"dt{m}", V.tensor_scalar(du[:, 0, m, :], p[:, :], bdts[:, m:m + 1], 0.0, ALU.add, ALU.max))
                for half in range(2):
                    for s in range(2):
                        r = 4 * i + 2 * half + s
                        yield SLOT["dt1"] + 7 + 6 * half + 3 * s
                        if s == 0:
                            v.wait_ge(ln_s, i + 1)
                            v.wait_ge(drained[BANK[f"dt{half}"]], t.before(f"dt{half}") + 1)
                            V.tensor_tensor(du[:, 0, half, :], du[:, 0, half, :], spa[:, half, :], ALU.add).then_inc(du_s, 1)
                        else:
                            v.wait_ge(du_s, r)
                            v.wait_ge(silu_s, 4 * i + half + 1)
                            V.tensor_tensor(du[:, 1, half, :], du[:, 0, half, :], xs[:, half, :], ALU.mult).then_inc(du_s, 1)
                        yield SLOT["dt1"] + 9 + 6 * half + 3 * s
                        v.wait_ge(hi_s, r + 1)
                        if not known(r, 1):
                            v.wait_ge(lo_s, r)
                        V.tensor_tensor(rest[:, :], du[:, s, half, :], parts[:, s, 0, half, :], ALU.subtract).then_inc(rest_s, 1)
                        yield SLOT["dt1"] + 11 + 6 * half + 3 * s
                        v.wait_ge(mid_s, r + 1)
                        V.tensor_tensor(parts[:, s, 2, half, :], rest[:, :], parts[:, s, 1, half, :], ALU.subtract).then_inc(lo_s, 1)
                for m in range(2):
                    v.wait_ge(drained[BANK[f"C{m}"]], t.before(f"C{m}") + 1)

            def take_sums(b, half, t, at):
                yield at
                v.wait_ge(summed, PAIRS // 4 * b + HALF // 4 * (half + 1))
                v.wait_ge(gate_ready, 4 * b + 4)
                if not known(2 * b + half, 1):
                    v.wait_ge(y3_s, 2 * b + half)
                V.tensor_tensor(yt[:, :], ys[:, :], cg[:, half, :], ALU.mult).then_inc(ys_taken, 1)
                yield at + 1
                v.wait_ge(ys_taken, 2 * b + half + 1)
                if half == 0 and t.post:
                    v.wait_ge(filled[BANK["z"]], t.before("z") + 1)
                V.tensor_tensor(y3[:, half, :], yt[:, :], xd[:, half, :], ALU.add).then_inc(y3_s, 1)

            def pre_b(t):
                b = t.b
                yield 6
                if not known(b, 1):
                    v.wait_ge(y3_s, 2 * b)
                v.wait_ge(silu_s, 4 * b + 4)
                for half in range(2):
                    V.tensor_tensor(cg[:, half, :], cm[:, half, :], sres[:, half, :], ALU.mult).then_inc(gate_ready, 1)
                    V.scalar_tensor_tensor(xd[:, half, :], xs[:, half, :], dps_[:, half:half + 1], sres[:, half, :],
                                           ALU.mult, ALU.mult).then_inc(gate_ready, 1)
                yield 12
                if t.post:
                    v.wait_ge(x1_s, b)
                v.wait_ge(nrm_s[0], 4 * b + 4)
                V.tensor_tensor(resa[:, :, :], xn[:, :, :], bcs[:, 0:1, :].to_broadcast([128, TT, D]), ALU.add).then_inc(res_ready, 1)
                V.tensor_tensor(resb[:, :, :], xnew[:, :, :], bcs[:, 2:3, :].to_broadcast([128, TT, D]), ALU.add).then_inc(res_ready, 1)

            def routing(t, m):
                c = t.b - 1
                yield SLOT[f"lg{m}"] + 1
                p = got(t, f"lg{m}")
                drain(f"lg{m}", V.tensor_copy(lg[:, :, :].rearrange("p a e -> p (a e)"), p[:, 0:TT * E]))
                v.wait_ge(drained[BANK[f"lg{m}"]], t.before(f"lg{m}") + 1)
                done = [0]
                r0 = ROUTE * (2 * c + m - 1)

                def link(ins):
                    done[0] += 1
                    ins.then_inc(route, 1)
                    v.wait_ge(route, r0 + done[0])

                R = lambda n: rt[:, n, :, :]
                def bc(n):
                    return rc[:, n, :].unsqueeze(2).to_broadcast([128, TT, E])
                revb = rev[:, :].unsqueeze(1).to_broadcast([128, TT, E])
                src = lg[:, :, :]
                for n in range(2):
                    link(V.tensor_reduce(rc[:, n, :], src, AX_X, ALU.max))
                    link(V.tensor_tensor(R(0), src, bc(n), ALU.is_equal))
                    link(V.tensor_tensor(R(0), R(0), revb, ALU.mult))
                    link(V.tensor_reduce(rc[:, 2 + n, :], R(0), AX_X, ALU.max))
                    link(V.tensor_tensor(R(1 + n), R(0), bc(2 + n), ALU.is_equal))
                    if n == 0:
                        link(V.scalar_tensor_tensor(R(3), R(1), LOWEST, lg[:, :, :], ALU.mult, ALU.add))
                        src = R(3)
                        yield SLOT[f"lg{m}"] + 2
                V.tensor_tensor(rc[:, 4, :], rc[:, 1, :], rc[:, 0, :], ALU.subtract).then_inc(gap_s, 1)
                yield SLOT[f"lg{m}"] + 6
                v.wait_ge(gap_e, 2 * c + m)
                link(V.tensor_scalar(rc[:, 6, :], rc[:, 5, :], 1.0, 2.0, ALU.add, ALU.mult))
                link(V.reciprocal(rc[:, 6, :], rc[:, 6, :]))
                link(V.tensor_tensor(rc[:, 7, :], rc[:, 6, :], rc[:, 5, :], ALU.mult))
                link(V.tensor_tensor(R(4), R(1), bc(6), ALU.mult))
                link(V.tensor_tensor(R(5), R(2), bc(7), ALU.mult))
                link(V.tensor_tensor(R(4), R(4), R(5), ALU.add))
                assert done[0] == ROUTE

            def moe_tiles(t, m):
                c = t.b - 1
                n0 = (TT - 1) * E * (2 * c + m - 1)
                for slot, name, n in MOE_V:
                    yield MOE_AT[m] + slot
                    if name == "h":
                        p = got(t, f"h{m}_{n}")
                        v.wait_ge(tanh_s, 4 * E * c + 2 * E * (m - 1) + n + 1)
                        drain(f"h{m}_{n}", V.scalar_tensor_tensor(sq[:, n % 2, :], tq[:, n % 2, :], 1.0, p[:, :],
                                                                  ALU.add, ALU.mult))
                    elif name == "g":
                        p = got(t, f"g{m}_{n}")
                        v.wait_ge(drained[BANK[f"h{m}_{n}"]], t.before(f"h{m}_{n}") + 1)
                        if n >= 4:
                            v.wait_ge(filled["Y"], t.before(f"y{m}_{n // 2 - 2}") + 1)
                        drain(f"g{m}_{n}", V.tensor_tensor(aq[:, n % 4, :], sq[:, n % 2, :], p[:, :], ALU.mult))
                    else:
                        p = got(t, f"y{m}_{n}")
                        if n >= 1:
                            v.wait_ge(added, n0 + (TT - 1) * n)
                            v.wait_ge(drained["Y"], t.before(f"y{m}_{n - 1}") + 1)
                        for a in range(TT):
                            ins = V.scalar_tensor_tensor(x1[:, a, :], p[:, a * 128:(a + 1) * 128], rt[:, 4, a, n:n + 1],
                                                         x1[:, a, :], ALU.mult, ALU.add)
                            if a < TT - 1:
                                ins.then_inc(added, 1)
                        drain(f"y{m}_{n}", ins)
                v.wait_ge(added, n0 + (TT - 1) * E)
                v.wait_ge(drained["Y"], t.before(f"y{m}_{E - 1}") + 1)

            def post(t):
                c = t.b - 1
                yield from take_sums(c, 1, t, 2)
                yield SLOT["z"] + 2
                p = got(t, "z")
                v.wait_ge(res_ready, 2 * c + 2)
                drain("z", V.tensor_tensor(z[:, :, :].rearrange("p a c -> p (a c)"), p[:, :],
                                           resa[:, :, :].rearrange("p a c -> p (a c)"), ALU.add))
                v.wait_ge(drained[BANK["z"]], t.before("z") + 1)
                yield from layer_norm(1, c, LN_AT[1], z, nrm)
                yield LN_AT[1] + 4
                v.wait_ge(nrm_s[1], 4 * c + 4)
                V.tensor_tensor(nrm[:, :, :], nrm[:, :, :], bcs[:, 1:2, :].to_broadcast([128, TT, D]), ALU.mult).then_inc(zg_s, 1)
                yield LN_AT[1] + 4
                v.wait_ge(zg_s, c + 1)
                v.wait_ge(x_out, 16 * c + 16)
                V.tensor_tensor(x1[:, :, :], nrm[:, :, :], resb[:, :, :], ALU.add).then_inc(x1_s, 1)
                v.wait_ge(x1_s, c + 1)
                yield from layer_norm(2, c, LN_AT[2], x1, nrm)
                yield from both(moe_tiles(t, 1), routing(t, 1))
                flat = lambda ap: ap[:, :, :].rearrange("p a c -> p (a c)")
                yield from layer_norm(3, c, LN_AT[3], x1, nrm)
                yield SLOT["P1"] + 1
                p1, p2 = got(t, "P1"), got(t, "P2")
                drain("P1", V.tensor_tensor(zt[2], p1[:, :], cosT[:, :], ALU.mult))
                drain("P2", V.tensor_tensor(zt[3], p2[:, :], sinT[:, :], ALU.mult))
                yield SLOT["P1"] + 2
                v.wait_ge(drained[BANK["P1"]], t.before("P1") + 1)
                v.wait_ge(drained[BANK["P2"]], t.before("P2") + 1)
                V.tensor_tensor(zt[2], zt[2], zt[3], ALU.add).then_inc(zb_s, 1)
                yield SLOT["P1"] + 3
                v.wait_ge(zb_s, c + 1)
                V.tensor_tensor_scan(zt[3], rT[:, :], zt[2], 0.0, ALU.mult, ALU.add).then_inc(zs_s, 1)
                yield SLOT["P1"] + 4
                v.wait_ge(zs_s, c + 1)
                V.tensor_tensor(zt[0], zt[3], cosT[:, :], ALU.mult).then_inc(q1_s, 1)
                yield SLOT["P1"] + 5
                V.tensor_tensor(zt[1], zt[3], sinT[:, :], ALU.mult).then_inc(q2_s, 1)
                yield SLOT["s5"] + 1
                p = got(t, "s5")
                drain("s5", V.scalar_tensor_tensor(yT[:, :], nT[:, :], sdt[:, 0:1], p[:, :], ALU.mult, ALU.add))
                yield SLOT["s5t"] + 1
                p = got(t, "s5t")
                drain("s5t", V.tensor_tensor(flat(x1), flat(x1), p[:, :], ALU.add))
                v.wait_ge(drained[BANK["s5t"]], t.before("s5t") + 1)
                yield from layer_norm(4, c, LN_AT[4], x1, nrm)
                yield from both(moe_tiles(t, 2), routing(t, 2))
                v.sem_inc(x4_s, 1)

            def scan(t):
                K = PAIRS * t.b

                def pair(k):
                    v.wait_ge(da, K + k + 1)
                    v.wait_ge(wq, K + k + 1)
                    if not known(K + k, H_RING):
                        v.wait_ge(summed, (PAIRS // 4) * t.b + (k - H_RING) // 4 + 1)
                    V.tensor_tensor_scan(h[:, k % H_RING, :], dtp[k % D_RING][:, :], w[:, k % W_RING, :], 0.0,
                                         ALU.mult, ALU.add).then_inc(scanned, 1)

                weave(pair, [pre_b(t), take_sums(t.b, 0, t, HALF + SUM_AT - 1)] + tasks_of(t, pre_a, post))

            turns(v, pre_a, scan, post)


_INS = ['L0_attn_a_x', 'L0_attn_a_Wi', 'L0_attn_a_bi', 'L0_attn_a_Wx', 'L0_attn_a_bx', 'L0_attn_a_Wdt', 'L0_attn_a_bdt',
        'L0_attn_a_A_log', 'L0_attn_a_Dp', 'L0_attn_a_Wo', 'L0_attn_a_bo', 'L0_attn_a_gamma', 'L0_attn_a_beta',
        'L0_attn_b_Lambda_re', 'L0_attn_b_Lambda_im', 'L0_attn_b_B', 'L0_attn_b_C', 'L0_attn_b_D', 'L0_attn_b_log_step',
        'L0_ffn_Wg', 'L0_ffn_W1', 'L0_ffn_W2', 'L0_ffn_W3']


def kernel(**inputs):
    import ml_dtypes
    import numpy as _np
    import concourse.bacc as _bacc
    from concourse import mybir as _mybir
    from concourse.bass_utils import run_bass_kernel_spmd as _run

    i, r, col = _np.arange(16)[None, :, None], _np.arange(96)[:, None, None] % 32, _np.arange(128)[None, None, :]
    sel = (r == 2 * i + col // 64).astype(ml_dtypes.bfloat16).reshape(96, 16 * 128)
    p, c32 = _np.arange(128)[:, None, None], _np.arange(32)[None, None, :]
    wsum = (c32 == 2 * i + p // 64).astype(_np.float32).reshape(128, 16 * 32)
    rev = _np.broadcast_to(8.0 - _np.arange(8), (128, 8)).astype(_np.float32)
    constants = {"c_ident": _np.eye(128, dtype=_np.float32), "c_sel": sel, "c_wsum": wsum, "c_rev": rev}

    nc = _bacc.Bacc("TRN2", target_bir_lowering=False, num_devices=1)
    arrays, args = {}, []
    for name, a in [(n, inputs[n]) for n in _INS] + list(constants.items()):
        a = _np.ascontiguousarray(a)
        arrays[f"in_{name}_dram"] = a
        args.append(nc.dram_tensor(f"in_{name}_dram", a.shape, _mybir.dt.from_np(a.dtype), kind="ExternalInput").ap())
    args.append(nc.dram_tensor("out_0_dram", (8, 512, 128), _mybir.dt.float32, kind="ExternalOutput").ap())
    hybrid_kernel(nc, *args)
    r = _run(nc, [arrays], core_ids=[0])
    return r.results[0]["out_0_dram"]
```

```python
from contextlib import ExitStack

import concourse.bass as bass
from concourse import mybir

ALU = mybir.AluOpType
ACT = mybir.ActivationFunctionType
F32 = mybir.dt.float32
BF16 = mybir.dt.bfloat16
I32 = mybir.dt.int32
AX_X = mybir.AxisListType.X

NB, L, D = 8, 512, 128
DI, NS = 256, 64
E, HID = 8, 256
TT = L // 128
PAIRS = DI // 2
HALF = PAIRS // 2
QUADS, PER_QUAD = 4, 16
EPS = 1e-5
LOWEST = -1e30
D_RING, U_RING, W_RING, H_RING = 3, 8, 3, 8
SUM_AT = 6
U_AHEAD = U_RING - 1
Y_LAG = 5
ADD_LAG = 1
PI = 3.141592653589793

MOE_AT = {1: 18, 2: 86}
QUARTER_SLOTS = {1: 9, 2: 9}


def tile_at(m, j):
    return QUARTER_SLOTS[m] * j // 4


def output_at(m, e):
    return tile_at(m, 2 * e + 1) + 1 + Y_LAG


S5_AT = MOE_AT[1] + output_at(1, E - 1) + ADD_LAG + 1
GATES_AT, RES_AT = 24, 36
MATRICES_AT = 46
PRE_AT = 61
LN_AT = [PRE_AT - 6, 7, 11, S5_AT, MOE_AT[2] - 7]
ROUTE = 17
EARLY_LOADS, LATE_LOADS = 23, 15
PE_STEPS = [
    (5, "post", "Y", "z"), (17, "post", "Y", "x1T"), (MOE_AT[1], "post", "Y", "lg1"),
    (S5_AT + 6, "post", "Y", "uT"), (S5_AT + 9, "post", "H", "P1"), (S5_AT + 9, "post", "G", "P2"),
    (S5_AT + 16, "post", "H", "s5"), (S5_AT + 19, "post", "Y", "s5t"),
    (MOE_AT[2] - 2, "post", "Y", "x3T"), (MOE_AT[2], "post", "Y", "lg2"),
] + [(PRE_AT + _n, "pre", _b, _name) for _n, _b, _name in (
    (0, "H", "xnT"), (2, "G", "in0"), (3, "X", "in1"), (4, "H", "in2"), (5, "G", "in3"), (9, "X", "draw"),
    (10, "H", "Bp"), (11, "G", "C0"), (12, "X", "C1"), (16, "G", "dt0"), (17, "X", "dt1"))]
for _m, _s in MOE_AT.items():
    PE_STEPS += [(_s + tile_at(_m, _j), "post", "HGX"[2 * _j % 3], f"h{_m}_{_j}") for _j in range(2 * E)]
    PE_STEPS += [(_s + tile_at(_m, _j) + 1, "post", "HGX"[(2 * _j + 1) % 3], f"g{_m}_{_j}") for _j in range(2 * E)]
    PE_STEPS += [(_s + output_at(_m, _e), "post", "Y", f"y{_m}_{_e}") for _e in range(E)]
PE_STEPS.sort(key=lambda s: (s[0], s[1] != "post"))
SLOT = {name: slot for slot, _, _, name in PE_STEPS}
BANK = {name: bank for _, _, bank, name in PE_STEPS}


def last_user(k, ring):
    return k - ring if k >= ring else max(j for j in range(PAIRS) if j % ring == k % ring) - PAIRS


def moe_pe(m):
    return sorted([(MOE_AT[m], "lg", 0)] + [(MOE_AT[m] + tile_at(m, j), "h", j) for j in range(2 * E)]
                  + [(MOE_AT[m] + tile_at(m, j) + 1, "g", j) for j in range(2 * E)]
                  + [(MOE_AT[m] + output_at(m, e), "y", e) for e in range(E)], key=lambda s: s[0])


def moe_v(m):
    return sorted([(MOE_AT[m] + tile_at(m, j) + 1, "h", j) for j in range(2 * E)]
                  + [(MOE_AT[m] + tile_at(m, j) + 2, "g", j) for j in range(2 * E)]
                  + [(MOE_AT[m] + output_at(m, e) + 1 + ADD_LAG, "y", e) for e in range(E)], key=lambda s: s[0])


class Turn:

    def __init__(self, b, pre, post, pres, posts):
        self.b, self.pre, self.post, self.pres, self.posts = b, pre, post, pres, posts

    def before(self, name):
        bank = BANK[name]
        steps = [s for s in PE_STEPS if s[2] == bank]
        per = {kind: sum(s[1] == kind for s in steps) for kind in ("pre", "post")}
        here = [s[3] for s in steps if (s[1] == "pre" and self.pre) or (s[1] == "post" and self.post)]
        return 1 + self.pres * per["pre"] + self.posts * per["post"] + here.index(name)


def both(one, other):
    left = [[next(g), g] for g in (one, other)]
    while left:
        first = min(left, key=lambda n: n[0])
        yield first[0]
        first[0] = next(first[1], None)
        left = [n for n in left if n[0] is not None]


def known(n, below):
    return isinstance(n, int) and n < below


def weave(pair, tasks):
    todo = [[t, next(t, None)] for t in tasks]
    for slot in range(PAIRS if pair else 0):
        pair(slot)
        for t in todo:
            while t[1] is not None and t[1] <= slot:
                t[1] = next(t[0], None)
    while any(t[1] is not None for t in todo):
        t = min((t for t in todo if t[1] is not None), key=lambda t: t[1])
        t[1] = next(t[0], None)


def hybrid_kernel(nc, x, Wi, bi, Wx, bx, Wdt, bdt, A_log, Dp, Wo, bo, gamma, beta, Lre, Lim, SB, SC, SD, log_step,
                  Wg, W1, W2, W3, c_ident, c_sel, c_wsum, c_rev, u_rows, out):
    with ExitStack() as ctx:
        def sb(name, shape, dt=F32):
            return ctx.enter_context(nc.sbuf_tensor(name, shape, dt))

        def sem(name):
            return ctx.enter_context(nc.semaphore(name))

        wi = sb("wi", [128, 2 * DI]); wx = sb("wx", [128, 2, 2 * NS + DI]); wxb = sb("wxb", [128, 2, 128])
        wdt = sb("wdt", [NS, DI]); wo = sb("wo", [128, 2, D]); wg = sb("wg", [128, E])
        w1 = sb("w1", [128, E, HID]); w2 = sb("w2", [128, E, HID]); w3 = sb("w3", [128, E, 2, D])
        ident = sb("ident", [128, 128])
        sel = sb("sel", [96, PER_QUAD, 128], BF16)
        wsum = sb("wsum", [128, PER_QUAD, 32])
        rev = sb("rev", [128, E])
        hbi = sb("hbi", [128, 4]); bxd = sb("bxd", [NS, 1]); bxb = sb("bxb", [128, 1]); bxc = sb("bxc", [128, 2])
        bdts = sb("bdts", [128, 2]); dps_ = sb("dps_", [128, 2]); rows = sb("rows", [1, 3, D]); bcs = sb("bcs", [128, 3, D])
        ones1 = sb("ones1", [1, 128]); one_col = sb("one_col", [128, 1]); mhalf = sb("mhalf", [128, TT])
        al = sb("al", [128, 128]); nega = sb("nega", [128, 128])
        s5p = sb("s5p", [128, 3]); s5w = sb("s5w", [128, 32]); s5i = sb("s5i", [128, 1], I32)
        sbt = sb("sbt", [NS, D, 2]); sct = sb("sct", [128, NS, 2]); bb = sb("bb", [NS, 4, D])
        cc = sb("cc", [128, 2, 2, NS]); mb = sb("mb", [128, 2, 128]); mc = sb("mc", [128, 2, 128])
        cosT = sb("cosT", [128, L]); sinT = sb("sinT", [128, L]); rT = sb("rT", [128, L]); sdt = sb("sdt", [128, 1])
        xnew = sb("xnew", [128, TT, D]); xn = sb("xn", [128, TT, D]); xnT = sb("xnT", [128, L])
        th = sb("th", [128, 2, L]); vh = sb("vh", [128, 2, L]); xs = sb("xs", [128, 2, L]); sres = sb("sres", [128, 2, L])
        draw = sb("draw", [NS, L]); btmp = sb("btmp", [128, L]); cm = sb("cm", [128, 2, L])
        spa = sb("spa", [128, 2, L]); du = sb("du", [128, 2, 2, L])
        rest = sb("rest", [128, L]); parts = sb("parts", [128, 3, 2, L], BF16)
        pdu = sb("pdu", [96, 8, L], BF16); bdup = sb("bdup", [128, L])
        cg = sb("cg", [128, 2, L]); xd = sb("xd", [128, 2, L]); resa = sb("resa", [128, TT, D]); resb = sb("resb", [128, TT, D])
        ub = sb("ub", [128, U_RING, L]); w = sb("w", [128, W_RING, L]); h = sb("h", [128, H_RING, L])
        yt = sb("yt", [128, L]); y3 = sb("y3", [128, 2, L])
        z = sb("z", [128, TT, D]); x1 = sb("x1", [128, TT, D]); nrm = sb("nrm", [128, TT, D]); nT = sb("nT", [128, L])
        bst = sb("bst", [128, 5, TT, 6]); bag = sb("bag", [128, 5, TT, 2]); var = sb("var", [128, 5, TT]); rs = sb("rs", [128, 5, TT])
        lg = sb("lg", [128, TT, E]); rt = sb("rt", [128, 8, TT, E]); rc = sb("rc", [128, 8, TT])
        tq = sb("tq", [128, 2, L]); sq = sb("sq", [128, 2, L]); aq = sb("aq", [128, 4, L])
        yT = sb("yT", [128, L])
        zt = [tq[:, 0, :], tq[:, 1, :], sq[:, 0, :], sq[:, 1, :]]

        banks = {n: ctx.enter_context(nc.psum_tensor("bank" + n, [128, 512], F32)) for n in "HGXY"}
        dtp = [ctx.enter_context(nc.psum_tensor(f"dtp{j}", [128, 512], F32)) for j in range(D_RING)]
        ys = ctx.enter_context(nc.psum_tensor("ys", [128, 512], F32))

        filled = {n: sem("filled" + n) for n in "HGXY"}
        drained = {n: sem("drained" + n) for n in "HGXY"}
        loads = sem("loads"); late_loads = sem("late_loads"); x_in = sem("x_in"); x_out = sem("x_out")
        ones_ready = sem("ones_ready"); angles_ready = sem("angles_ready"); matrices_ready = sem("matrices_ready")
        setup_done = sem("setup_done"); setup_chain = sem("setup_chain"); rows_spread = sem("rows_spread")
        matrices_turned = sem("matrices_turned"); setup_a = sem("setup_a"); diagonal_a = sem("diagonal_a")
        parts_in = [sem("parts_in0"), sem("parts_in1")]
        decay_spread = sem("decay_spread"); input_spread = [sem(f"input_spread{j}") for j in range(U_RING)]; inputs_stored = [sem("u_stored0"), sem("u_stored1")]; decay_ready = sem("decay_ready"); product_ready = sem("product_ready")
        scanned = sem("scanned"); summed = sem("summed"); ys_taken = sem("ys_taken")
        b_ready = sem("b_ready"); gate_ready = sem("gate_ready"); direct_ready = sem("direct_ready"); c_ready = sem("c_ready"); res_ready = sem("res_ready")
        stats_ready = [sem(f"stats_ready{k}") for k in range(5)]; moments_ready = [sem(f"moments_ready{k}") for k in range(5)]; variance_ready = [sem(f"variance_ready{k}") for k in range(5)]
        rstd_ready = [sem(f"rstd_ready{k}") for k in range(5)]; normed = [sem(f"normed{k}") for k in range(5)]
        tanh_ready = sem("tanh_ready"); silu_ready = sem("silu_ready"); abs_ready = sem("abs_ready"); exp_ready = sem("exp_ready"); log_ready = sem("log_ready")
        steps_ready = sem("steps_ready"); high_part_ready = sem("high_part_ready"); middle_part_ready = sem("middle_part_ready"); rest_ready = sem("rest_ready"); low_part_ready = sem("low_part_ready")
        gated_ready = sem("gated_ready"); scaled_ready = sem("scaled_ready"); x1_ready = sem("x1_ready")
        gap_ready = sem("gap_ready"); gap_exp_ready = sem("gap_exp_ready"); routed = sem("routed")
        hidden_tanh_ready = sem("hidden_tanh_ready"); added = sem("added")
        turned_ready = sem("turned_ready"); diagonal_scanned = sem("diagonal_scanned"); real_ready = sem("real_ready"); imaginary_ready = sem("imaginary_ready")
        sequence_done = sem("sequence_done")

        block = ctx.enter_context(nc.Block())

        def turns(eng, pre_a, scan, post):
            weave(None, [pre_a(Turn(-1, True, False, 0, 0))])
            scan(Turn(0, True, False, 1, 0))
            with eng.Fori(1, NB - 1) as b:
                scan(Turn(b, True, True, b + 1, b - 1))
            scan(Turn(NB - 1, False, True, NB, NB - 2))
            weave(None, [post(Turn(NB, False, True, NB, NB - 1))])

        def tasks_of(t, pre_a, post, extra=()):
            return ([post(t)] if t.post else []) + ([pre_a(t)] if t.pre else []) + list(extra)

        @block.sync
        def _(sp):
            sp.sem_inc(x_out, 16)
            loaded = []

            def load(dst, src):
                loaded.append(sp.dma_start(dst, src).then_inc(loads if len(loaded) < EARLY_LOADS else late_loads, 16))

            def load_columns(dst, src, at, n):
                for m in range(n):
                    load(dst[:, m:m + 1], src[at + 128 * m:at + 128 * (m + 1)].rearrange("(p a) -> p a", a=1))

            load(ident[:, :], c_ident)
            load(wi[:, :], Wi)
            load_columns(hbi, bi, 0, 4)
            sp.dma_start(xnew[:, :, :], x[0].rearrange("(a p) c -> p a c", p=128)).then_inc(x_in, 16)
            load(wx[:, :, :], Wx.rearrange("(k p) n -> p k n", p=128))
            load(wdt[:, :], Wdt)
            load(bxd[:, :], bx[0:NS].rearrange("(p a) -> p a", a=1))
            for j in range(2):
                load(bxb[64 * j:64 * j + 64, :], bx[NS:2 * NS].rearrange("(p a) -> p a", a=1))
            load_columns(bxc, bx, 2 * NS, 2)
            load_columns(bdts, bdt, 0, 2)
            load_columns(dps_, Dp, 0, 2)
            load(al[:, :], A_log.rearrange("(d j) n -> d (j n)", j=2))
            load(sel[:, :, :], c_sel.rearrange("k (i m) -> k i m", m=128))
            load(wsum[:, :, :], c_wsum.rearrange("k (i m) -> k i m", m=32))
            for n, v in enumerate((bo, gamma, beta)):
                load(rows[:, n, :], v.rearrange("(a n) -> a n", a=1))
            assert len(loaded) == EARLY_LOADS
            for j in range(2):
                for n, v in enumerate((Lre.rearrange("(p a) -> p a", a=1), Lim.rearrange("(p a) -> p a", a=1), log_step)):
                    load(s5p[64 * j:64 * j + 64, n:n + 1], v)
            load(sbt[:, :, :], SB)
            load(sct[:, :, :], SC)
            load(sdt[:, :], SD.rearrange("(p a) -> p a", a=1))
            load(wo[:, :, :], Wo.rearrange("(k p) n -> p k n", p=128))
            load(wg[:, :], Wg)
            load(rev[:, :], c_rev)
            load(w1[:, :, :], W1.rearrange("e c h -> c e h"))
            load(w2[:, :, :], W2.rearrange("e c h -> c e h"))
            load(w3[:, :, :, :], W3.rearrange("e (k p) c -> p e k c", p=128))

            assert len(loaded) == EARLY_LOADS + LATE_LOADS

            def send_parts(i, half):
                sp.wait_ge(low_part_ready, 2 * i + half + 1)
                sp.nop(nofuse=True)
                for part in range(3):
                    for q in range(QUADS):
                        sp.dma_start(pdu[32 * part:32 * part + 32, 4 * half + q, :],
                                     parts[32 * q:32 * q + 32, part, half, :]).then_inc(parts_in[half], 16)

            def store_inputs(i, half):
                sp.wait_ge(steps_ready, 4 * i + 2 * half + 2)
                sp.nop(nofuse=True)
                sp.dma_start(u_rows[i, 128 * half:128 * half + 128, :], du[:, 1, half, :]).then_inc(inputs_stored[half], 16)

            def spread_input(i, k):
                half, n, q = k // HALF, (k % HALF) // 4, k % 4
                c = 128 * half + 32 * q + 2 * n
                if k % HALF == 0:
                    sp.wait_ge(inputs_stored[half], 16 * i + 16)
                    sp.nop(nofuse=True)
                if not known(PAIRS * i + k, U_RING):
                    sp.wait_ge(product_ready, PAIRS * i + k - U_RING + 1)
                    sp.nop(nofuse=True)
                sp.dma_start(ub[:, k % U_RING, :], u_rows[i, c:c + 2, :].unsqueeze(1).to_broadcast([2, NS, L]))\
                    .then_inc(input_spread[k % U_RING], 16)

            def pre_a(t):
                i = t.b + 1
                if not known(t.b, 0):
                    yield PRE_AT - 12
                    sp.wait_ge(res_ready, 2 * i)
                    sp.nop(nofuse=True)
                    sp.dma_start(xnew[:, :, :], x[i].rearrange("(a p) c -> p a c", p=128)).then_inc(x_in, 16)
                    yield SLOT["dt1"] + 14
                    sp.wait_ge(decay_spread, PAIRS * t.b + HALF)
                    sp.nop(nofuse=True)
                else:
                    yield 0
                send_parts(i, 0)
                store_inputs(i, 0)
                yield SLOT["dt1"] + 20
                store_inputs(i, 1)

            def post(t):
                c = t.b - 1
                yield PAIRS - 1
                sp.wait_ge(sequence_done, c + 1)
                sp.nop(nofuse=True)
                sp.dma_start(out[c].rearrange("(a p) c -> p a c", p=128), x1[:, :, :]).then_inc(x_out, 16)

            def scan(t):
                def pair(k):
                    if k == 0:
                        if not known(t.b, 1):
                            sp.wait_ge(decay_spread, PAIRS * t.b)
                            sp.nop(nofuse=True)
                        send_parts(t.b, 1)
                    if k + U_AHEAD < PAIRS:
                        spread_input(t.b, k + U_AHEAD)
                    elif t.pre:
                        spread_input(t.b + 1, k + U_AHEAD - PAIRS)
                weave(pair, tasks_of(t, pre_a, post))

            weave(None, [pre_a(Turn(-1, True, False, 0, 0))])
            for k in range(U_AHEAD):
                spread_input(0, k)
            scan(Turn(0, True, False, 1, 0))
            with sp.Fori(1, NB - 1) as b:
                scan(Turn(b, True, True, b + 1, b - 1))
            scan(Turn(NB - 1, False, True, NB, NB - 2))
            weave(None, [post(Turn(NB, False, True, NB, NB - 1))])
            sp.wait_ge(x_out, 16 * NB + 16)

        @block.tensor
        def _(pe):
            def claim(t, name):
                pe.wait_ge(drained[BANK[name]], t.before(name))
                return banks[BANK[name]]

            def is_filled(t, name, ins):
                ins.then_inc(filled[BANK[name]], 1)

            def turn_tiles(t, name, src):
                p = claim(t, name)
                for a in range(TT):
                    ins = nc.tensor.transpose(p[:, a * 128:(a + 1) * 128], src(a), ident[:, :])
                is_filled(t, name, ins)

            for n in "HGXY":
                pe.sem_inc(filled[n], 1)
            pe.wait_ge(loads, 16 * EARLY_LOADS)
            pe.wait_ge(setup_a, 1)
            nc.tensor.transpose(dtp[2][:, 0:128], al[:, :], ident[:, :])
            pe.wait_ge(ones_ready, 1)
            nc.tensor.matmul(dtp[0][:, 0:3 * D], ones1[:, :], rows[:, :, :].rearrange("a n c -> a (n c)"),
                             start=True, stop=True).then_inc(rows_spread, 1)
            pe.wait_ge(setup_done, 1)

            def diagonal_setup():
                yield MATRICES_AT
                pe.wait_ge(late_loads, 16 * LATE_LOADS)
                pe.wait_ge(matrices_ready, 1)
                for j in range(4):
                    nc.tensor.transpose(banks["Y"][:, j * 64:(j + 1) * 64], bb[:, j, :], ident[0:64, 0:64])
                for j in range(2):
                    ins = nc.tensor.transpose(banks["Y"][:, 256 + j * 128:256 + (j + 1) * 128], cc[:, j, :, :].rearrange("h c p -> h (c p)"), ident[:, :])
                ins.then_inc(matrices_turned, 1)

            def pre_a(t):
                i = t.b + 1
                yield SLOT["xnT"]
                pe.wait_ge(normed[0], 4 * i + 4)
                turn_tiles(t, "xnT", lambda a: xn[:, a, :])
                for m in range(4):
                    yield SLOT[f"in{m}"]
                    p = claim(t, f"in{m}")
                    if m == 0:
                        pe.wait_ge(drained[BANK["xnT"]], t.before("xnT") + 1)
                    is_filled(t, f"in{m}", nc.tensor.matmul(p[:, :], wi[:, m * 128:(m + 1) * 128], xnT[:, :],
                                                            start=True, stop=True))
                for name, lhs in (("draw", lambda k: wx[:, k, 0:NS]), ("Bp", lambda k: wxb[:, k, :]),
                                  ("C0", lambda k: wx[:, k, 2 * NS:2 * NS + 128]),
                                  ("C1", lambda k: wx[:, k, 2 * NS + 128:2 * NS + 256])):
                    yield SLOT[name]
                    p = claim(t, name)
                    if name == "draw":
                        pe.wait_ge(silu_ready, 4 * i + 2)
                    o = p[0:NS, :] if name == "draw" else p[:, :]
                    for k in range(2):
                        ins = nc.tensor.matmul(o, lhs(k), xs[:, k, :], start=(k == 0), stop=(k == 1))
                    is_filled(t, name, ins)
                for m in range(2):
                    yield SLOT[f"dt{m}"]
                    p = claim(t, f"dt{m}")
                    if m == 0:
                        pe.wait_ge(drained[BANK["draw"]], t.before("draw") + 1)
                    is_filled(t, f"dt{m}", nc.tensor.matmul(p[:, :], wdt[:, m * 128:(m + 1) * 128], draw[:, :],
                                                            start=True, stop=True))

            def moe(t, m):
                c = t.b - 1
                lnk = {1: 2, 2: 4}[m]
                yield SLOT[f"x{2 * m - 1}T"]
                pe.wait_ge(normed[lnk], 4 * c + 4)
                turn_tiles(t, f"x{2 * m - 1}T", lambda a: nrm[:, a, :])
                for slot, name, n in moe_pe(m):
                    yield slot
                    if name == "lg":
                        p = claim(t, f"lg{m}")
                        for a in range(TT):
                            ins = nc.tensor.matmul(p[:, a * E:(a + 1) * E], nT[:, a * 128:(a + 1) * 128], wg[:, :],
                                                   start=True, stop=True)
                        is_filled(t, f"lg{m}", ins)
                    elif name in "hg":
                        p, wt = claim(t, f"{name}{m}_{n}"), w1 if name == "h" else w2
                        is_filled(t, f"{name}{m}_{n}", nc.tensor.matmul(p[:, :], wt[:, n // 2, n % 2 * 128:n % 2 * 128 + 128],
                                                                        nT[:, :], start=True, stop=True))
                    else:
                        p = claim(t, f"y{m}_{n}")
                        for k in range(2):
                            pe.wait_ge(drained[BANK[f"g{m}_{2 * n + k}"]], t.before(f"g{m}_{2 * n + k}") + 1)
                        for a in range(TT):
                            for k in range(2):
                                ins = nc.tensor.matmul(p[:, a * 128:(a + 1) * 128], aq[:, (2 * n + k) % 4, a * 128:(a + 1) * 128],
                                                       w3[:, n, k, :], start=(k == 0), stop=(k == 1))
                        is_filled(t, f"y{m}_{n}", ins)

            def post(t):
                c = t.b - 1
                yield SLOT["z"]
                p = claim(t, "z")
                pe.wait_ge(gated_ready, 2 * c + 2)
                for a in range(TT):
                    for k in range(2):
                        ins = nc.tensor.matmul(p[:, a * 128:(a + 1) * 128], y3[:, k, a * 128:(a + 1) * 128], wo[:, k, :],
                                               start=(k == 0), stop=(k == 1))
                is_filled(t, "z", ins)
                yield from moe(t, 1)
                yield SLOT["uT"]
                pe.wait_ge(normed[3], 4 * c + 4)
                turn_tiles(t, "uT", lambda a: nrm[:, a, :])
                yield SLOT["P1"]
                for k, name in enumerate(("P1", "P2")):
                    p = claim(t, name)
                    if k == 0:
                        pe.wait_ge(drained[BANK["uT"]], t.before("uT") + 1)
                    is_filled(t, name, nc.tensor.matmul(p[:, :], mb[:, k, :], nT[:, :], start=True, stop=True))
                yield SLOT["s5"]
                p = claim(t, "s5")
                pe.wait_ge(real_ready, c + 1)
                nc.tensor.matmul(p[:, :], mc[:, 0, :], zt[0], start=True, stop=False)
                pe.wait_ge(imaginary_ready, c + 1)
                is_filled(t, "s5", nc.tensor.matmul(p[:, :], mc[:, 1, :], zt[1], start=False, stop=True))
                yield SLOT["s5t"]
                pe.wait_ge(drained[BANK["s5"]], t.before("s5") + 1)
                turn_tiles(t, "s5t", lambda a: yT[:, a * 128:(a + 1) * 128])
                yield from moe(t, 2)

            def scan(t):
                K = PAIRS * t.b

                def sum_states(group):
                    i, half = group % PER_QUAD, group // PER_QUAD
                    pe.wait_ge(scanned, K + 4 * group + 4)
                    if i == 0 and not known(K + group, 1):
                        pe.wait_ge(ys_taken, 2 * t.b + half)
                    for q in range(QUADS):
                        ins = nc.tensor.matmul(ys[32 * q:32 * q + 32, :], wsum[:, i, :], h[:, (4 * group + q) % H_RING, :],
                                               start=(i == 0), stop=(i == PER_QUAD - 1))
                    ins.then_inc(summed, 1)

                def pair(k):
                    i, q, half = (k % HALF) // 4, k % 4, k // HALF
                    if k % HALF == 0:
                        pe.wait_ge(parts_in[half], 192 * t.b + 192)
                    last = last_user(k, D_RING)
                    if not known(K + last, 0):
                        pe.wait_ge(scanned, K + last + 1)
                    nc.tensor.matmul(dtp[k % D_RING][:, :], sel[:, i, :], pdu[:, 4 * half + q, :],
                                     start=True, stop=True).then_inc(decay_spread, 1)
                    if k % 4 == SUM_AT % 4 and k >= SUM_AT:
                        sum_states((k - SUM_AT) // 4)

                def tail():
                    yield PAIRS
                    for group in range((PAIRS - 1 - SUM_AT) // 4 + 1, PAIRS // 4):
                        sum_states(group)

                weave(pair, [tail()] + tasks_of(t, pre_a, post, [diagonal_setup()] if known(t.b, 1) else []))

            turns(pe, pre_a, scan, post)

        @block.scalar
        def _(act):
            A = nc.scalar.activation

            def got(t, name):
                act.wait_ge(filled[BANK[name]], t.before(name) + 1)
                return banks[BANK[name]]

            def copy_out(t, name, dst, src=None, func=ACT.Copy, **kw):
                p = got(t, name)
                A(dst, p[:, :] if src is None else src(p), func, **kw).then_inc(drained[BANK[name]], 1)

            act.wait_ge(loads, 16 * EARLY_LOADS)
            A(al[:, :], al[:, :], ACT.Exp).then_inc(setup_a, 1)
            act.wait_ge(setup_done, 1)

            def diagonal_setup():
                yield 1
                act.wait_ge(late_loads, 16 * LATE_LOADS)
                A(s5w[:, 0:1], s5p[:, 2:3], ACT.Exp).then_inc(diagonal_a, 1)
                yield 8
                act.wait_ge(angles_ready, 1)
                A(s5w[:, 3:4], s5w[:, 2:3], ACT.Exp).then_inc(diagonal_a, 1)
                A(s5w[:, 6:7], s5w[:, 4:5], ACT.Sin).then_inc(diagonal_a, 1)
                A(s5w[:, 7:8], s5w[:, 5:6], ACT.Sin).then_inc(diagonal_a, 1)

            def pre_a(t):
                i = t.b + 1
                yield SLOT["xnT"] + 1
                copy_out(t, "xnT", xnT[:, :])
                for m in range(4):
                    yield SLOT[f"in{m}"] + 1
                    p = got(t, f"in{m}")
                    if m >= 2:
                        act.wait_ge(silu_ready, 4 * i + m - 1)
                    elif not known(i, 1):
                        act.wait_ge(silu_ready, 4 * i)
                    A(th[:, m % 2, :], p[:, :], ACT.Tanh, bias=hbi[:, m:m + 1], scale=0.5).then_inc(tanh_ready, 1)
                    A(vh[:, m % 2, :], p[:, :], ACT.Identity, bias=hbi[:, m:m + 1], scale=0.5)\
                        .then_inc(drained[BANK[f"in{m}"]], 1)
                yield SLOT["draw"] + 1
                copy_out(t, "draw", draw[:, :], lambda p: p[0:NS, :], ACT.Identity, bias=bxd[:, 0:1])
                yield SLOT["Bp"] + 1
                if not known(i, 1):
                    act.wait_ge(b_ready, i)
                    act.wait_ge(gate_ready, 2 * i)
                copy_out(t, "Bp", btmp[:, :], None, ACT.Identity, bias=bxb[:, 0:1])
                for m in range(2):
                    yield SLOT[f"C{m}"] + 1
                    copy_out(t, f"C{m}", cm[:, m, :], None, ACT.Identity, bias=bxc[:, m:m + 1])
                for m in range(2):
                    yield SLOT[f"dt{m}"] + 1
                    p = got(t, f"dt{m}")
                    if m == 0 and not known(i, 1):
                        act.wait_ge(steps_ready, 4 * i)
                    A(spa[:, m, :], p[:, :], ACT.Abs, bias=bdts[:, m:m + 1]).then_inc(abs_ready, 1)
                yield SLOT["dt1"] + 2
                act.wait_ge(abs_ready, 2 * i + 2)
                A(spa[:, :, :], spa[:, :, :], ACT.Exp, scale=-1.0).then_inc(exp_ready, 1)
                yield SLOT["dt1"] + 4
                act.wait_ge(exp_ready, i + 1)
                A(spa[:, :, :], spa[:, :, :], ACT.Ln, bias=one_col[:, 0:1]).then_inc(log_ready, 1)
                for half in range(2):
                    r = 2 * i + half
                    yield SLOT["dt1"] + 8 + 6 * half
                    act.wait_ge(steps_ready, 4 * i + 2 * half + 1)
                    if not known(i, 1):
                        act.wait_ge(parts_in[half], 192 * i)
                    A(parts[:, 0, half, :], du[:, 0, half, :], ACT.Copy).then_inc(high_part_ready, 1)
                    yield SLOT["dt1"] + 10 + 6 * half
                    act.wait_ge(rest_ready, r + 1)
                    A(parts[:, 1, half, :], rest[:, :], ACT.Copy).then_inc(middle_part_ready, 1)
                act.wait_ge(drained[BANK["Bp"]], t.before("Bp") + 1)

            def moe(t, m):
                c = t.b - 1
                yield SLOT[f"x{2 * m - 1}T"] + 1
                copy_out(t, f"x{2 * m - 1}T", nT[:, :])
                for j in range(2 * E):
                    yield SLOT[f"h{m}_{j}"] + 1
                    p = got(t, f"h{m}_{j}")
                    if j >= 2:
                        act.wait_ge(drained[BANK[f"h{m}_{j - 2}"]], t.before(f"h{m}_{j - 2}") + 1)
                    A(tq[:, j % 2, :], p[:, :], ACT.Tanh, scale=0.5).then_inc(hidden_tanh_ready, 1)
                    if j == 2:
                        act.wait_ge(gap_ready, 2 * c + m)
                        A(rc[:, 5, :], rc[:, 4, :], ACT.Exp).then_inc(gap_exp_ready, 1)

            def post(t):
                yield from moe(t, 1)
                yield SLOT["uT"] + 1
                copy_out(t, "uT", nT[:, :])
                yield from moe(t, 2)

            def scan(t):
                K = PAIRS * t.b

                def pair(k):
                    half, i, q = k // HALF, (k % HALF) // 4, k % 4
                    col = HALF * half + PER_QUAD * q + i
                    if k == 0:
                        if not known(K, 1):
                            act.wait_ge(product_ready, K)
                        A(bdup[:, :], btmp[:, :], ACT.Copy).then_inc(b_ready, 1)
                    act.wait_ge(decay_spread, K + k + 1)
                    A(dtp[k % D_RING][:, :], dtp[k % D_RING][:, :], ACT.Exp, scale=nega[:, col:col + 1]).then_inc(decay_ready, 1)

                weave(pair, tasks_of(t, pre_a, post, [diagonal_setup()] if known(t.b, 1) else []))

            turns(act, pre_a, scan, post)

        @block.gpsimd
        def _(pool):
            def rstd(k, i, at):
                yield at
                pool.wait_ge(variance_ready[k], i + 1)
                nc.gpsimd.tensor_tensor(rs[:, k, :], var[:, k, :], mhalf[:, :], ALU.pow).then_inc(rstd_ready[k], 1)

            pool.wait_ge(loads, 16 * EARLY_LOADS)
            pool.wait_ge(setup_done, 1)

            def pre_a(t):
                yield from rstd(0, t.b + 1, LN_AT[0] + 1)

            def post(t):
                for k in range(1, 5):
                    yield from rstd(k, t.b - 1, LN_AT[k] + 1)

            def gates(t):
                b = t.b
                for half in range(2):
                    yield GATES_AT + 2 + 3 * half
                    if half == 0:
                        if not known(b, 1):
                            pool.wait_ge(gated_ready, 2 * b)
                        pool.wait_ge(silu_ready, 4 * b + 4)
                        pool.wait_ge(c_ready, b + 1)
                    nc.gpsimd.tensor_tensor(cg[:, half, :], cm[:, half, :], sres[:, half, :], ALU.mult).then_inc(gate_ready, 1)
                yield RES_AT
                if t.post:
                    pool.wait_ge(x1_ready, b)
                pool.wait_ge(normed[0], 4 * b + 4)
                nc.gpsimd.tensor_tensor(resa[:, :, :], xn[:, :, :], bcs[:, 0:1, :].to_broadcast([128, TT, D]), ALU.add).then_inc(res_ready, 1)
                yield RES_AT + 3
                nc.gpsimd.tensor_tensor(resb[:, :, :], xnew[:, :, :], bcs[:, 2:3, :].to_broadcast([128, TT, D]), ALU.add).then_inc(res_ready, 1)

            def scan(t):
                K = PAIRS * t.b

                def pair(k):
                    if k == 0:
                        pool.wait_ge(b_ready, t.b + 1)
                    pool.wait_ge(input_spread[k % U_RING], 16 * (PAIRS // U_RING) * t.b + 16 * (k // U_RING) + 16)
                    last = last_user(k, W_RING)
                    if not known(K + last, 0):
                        pool.wait_ge(scanned, K + last + 1)
                    nc.gpsimd.tensor_tensor(w[:, k % W_RING, :], ub[:, k % U_RING, :], bdup[:, :], ALU.mult).then_inc(product_ready, 1)

                weave(pair, [gates(t)] + tasks_of(t, pre_a, post))

            turns(pool, pre_a, scan, post)

        @block.vector
        def _(v):
            V = nc.vector
            step = [0]

            def got(t, name):
                v.wait_ge(filled[BANK[name]], t.before(name) + 1)
                return banks[BANK[name]]

            def drain(name, ins):
                ins.then_inc(drained[BANK[name]], 1)

            def chain(ins):
                step[0] += 1
                ins.then_inc(setup_chain, 1)
                v.wait_ge(setup_chain, step[0])

            chain(V.memset(one_col[:, :], 1.0))
            chain(V.memset(mhalf[:, :], -0.5))
            chain(V.memset(ones1[:, :], 1.0))
            v.sem_inc(ones_ready, 1)
            v.wait_ge(loads, 16 * EARLY_LOADS)
            chain(V.tensor_scalar(hbi[:, :], hbi[:, :], 0.5, None, ALU.mult))
            for k in range(2):
                for j in range(2):
                    chain(V.tensor_copy(wxb[:, k, 64 * j:64 * j + 64], wx[:, k, NS:2 * NS]))
            v.wait_ge(rows_spread, 1)
            chain(V.tensor_scalar(nega[:, :], dtp[2][:, 0:128], -1.0, None, ALU.mult))
            chain(V.tensor_copy(bcs[:, :, :].rearrange("p n c -> p (n c)"), dtp[0][:, 0:3 * D]))
            for n in "HGX":
                v.sem_inc(drained[n], 1)
            v.sem_inc(setup_done, 1)

            def diagonal_setup():
                S = lambda n: s5w[:, n:n + 1]
                yield 2
                v.wait_ge(late_loads, 16 * LATE_LOADS)
                v.wait_ge(diagonal_a, 1)
                chain(V.tensor_scalar(S(1), s5p[:, 0:1], -1e-4, None, ALU.min))
                chain(V.tensor_tensor(S(2), S(1), S(0), ALU.mult))
                chain(V.tensor_tensor(S(8), s5p[:, 1:2], S(0), ALU.mult))
                yield 4
                chain(V.tensor_scalar(S(9), S(8), 1.0 / (2 * PI), None, ALU.mult))
                chain(V.tensor_copy(s5i[:, :], S(9)))
                chain(V.tensor_copy(S(10), s5i[:, :]))
                chain(V.scalar_tensor_tensor(S(8), S(10), -6.28125, S(8), ALU.mult, ALU.add))
                chain(V.scalar_tensor_tensor(S(8), S(10), -(2 * PI - 6.28125), S(8), ALU.mult, ALU.add))
                chain(V.tensor_scalar(S(4), S(8), 0.5, None, ALU.mult))
                chain(V.tensor_scalar(S(5), S(4), -1.0, None, ALU.mult))
                chain(V.tensor_tensor(S(5), S(4), S(5), ALU.max))
                chain(V.tensor_scalar(S(5), S(5), -1.0, PI / 2, ALU.mult, ALU.add))
                v.sem_inc(angles_ready, 1)
                yield 10
                v.wait_ge(diagonal_a, 4)
                c_, s_, er = S(11), S(12), S(3)
                chain(V.tensor_tensor(S(13), S(6), S(6), ALU.mult))
                chain(V.tensor_scalar(S(13), S(13), 2.0, None, ALU.mult))
                chain(V.tensor_scalar(c_, S(13), -1.0, 1.0, ALU.mult, ALU.add))
                chain(V.tensor_tensor(s_, S(6), S(7), ALU.mult))
                chain(V.tensor_scalar(s_, s_, 2.0, None, ALU.mult))
                yield 12
                chain(V.tensor_scalar(S(14), er, -1.0, None, ALU.add))
                chain(V.tensor_tensor(S(15), er, S(13), ALU.mult))
                chain(V.tensor_tensor(S(14), S(14), S(15), ALU.subtract))
                chain(V.tensor_tensor(S(15), er, s_, ALU.mult))
                chain(V.tensor_tensor(S(16), S(1), S(1), ALU.mult))
                chain(V.scalar_tensor_tensor(S(16), s5p[:, 1:2], s5p[:, 1:2], S(16), ALU.mult, ALU.add))
                yield 13
                chain(V.reciprocal(S(16), S(16)))
                chain(V.tensor_tensor(S(17), S(15), s5p[:, 1:2], ALU.mult))
                chain(V.scalar_tensor_tensor(S(17), S(14), S(1), S(17), ALU.mult, ALU.add))
                chain(V.tensor_tensor(S(17), S(17), S(16), ALU.mult))
                chain(V.tensor_tensor(S(18), S(14), s5p[:, 1:2], ALU.mult))
                chain(V.scalar_tensor_tensor(S(18), S(15), S(1), S(18), ALU.mult, ALU.subtract))
                chain(V.tensor_tensor(S(18), S(18), S(16), ALU.mult))
                yield 15
                fr, fi = s5w[0:NS, 17:18], s5w[0:NS, 18:19]
                chain(V.tensor_scalar(bb[:, 3, :], sbt[:, :, 1], fi, None, ALU.mult))
                chain(V.scalar_tensor_tensor(bb[:, 0, :], sbt[:, :, 0], fr, bb[:, 3, :], ALU.mult, ALU.subtract))
                chain(V.tensor_scalar(bb[:, 3, :], sbt[:, :, 0], fi, None, ALU.mult))
                chain(V.scalar_tensor_tensor(bb[:, 1, :], sbt[:, :, 1], fr, bb[:, 3, :], ALU.mult, ALU.add))
                yield 17
                chain(V.tensor_copy(bb[:, 2, :], bb[:, 1, :]))
                chain(V.tensor_scalar(bb[:, 3, :], bb[:, 0, :], -1.0, None, ALU.mult))
                yield 19
                chain(V.tensor_copy(cc[:, 0, 0, :], sct[:, :, 0]))
                chain(V.tensor_scalar(cc[:, 0, 1, :], sct[:, :, 1], -1.0, None, ALU.mult))
                chain(V.tensor_copy(cc[:, 1, 0, :], cc[:, 0, 1, :]))
                chain(V.tensor_scalar(cc[:, 1, 1, :], sct[:, :, 0], -1.0, None, ALU.mult))
                v.sem_inc(matrices_ready, 1)
                yield 21
                chain(V.memset(cosT[:, 0:1], 1.0))
                chain(V.memset(sinT[:, 0:1], 0.0))
                n = 1
                while n < L:
                    yield 22 + 2 * n.bit_length()
                    chain(V.tensor_scalar(rT[:, 0:n], sinT[:, 0:n], s_, None, ALU.mult))
                    chain(V.scalar_tensor_tensor(cosT[:, n:2 * n], cosT[:, 0:n], c_, rT[:, 0:n], ALU.mult, ALU.subtract))
                    chain(V.tensor_scalar(rT[:, 0:n], cosT[:, 0:n], s_, None, ALU.mult))
                    chain(V.scalar_tensor_tensor(sinT[:, n:2 * n], sinT[:, 0:n], c_, rT[:, 0:n], ALU.mult, ALU.add))
                    yield 23 + 2 * n.bit_length()
                    chain(V.tensor_tensor(S(19), s_, s_, ALU.mult))
                    chain(V.tensor_tensor(S(20), c_, s_, ALU.mult))
                    chain(V.tensor_tensor(S(21), c_, c_, ALU.mult))
                    chain(V.tensor_tensor(c_, S(21), S(19), ALU.subtract))
                    chain(V.tensor_scalar(s_, S(20), 2.0, None, ALU.mult))
                    n *= 2
                chain(V.tensor_scalar(rT[:, :], cosT[:, :], 0.0, er, ALU.mult, ALU.add))
                yield MATRICES_AT + 2
                v.wait_ge(matrices_turned, 1)
                chain(V.tensor_copy(mb[:, :, :].rearrange("p n c -> p (n c)"), banks["Y"][:, 0:256]))
                chain(V.tensor_copy(mc[:, :, :].rearrange("p n c -> p (n c)"), banks["Y"][:, 256:512]))
                v.sem_inc(drained["Y"], 1)

            def layer_norm(k, i, at, src, dst):
                yield at
                for a in range(TT):
                    ins = V.bn_stats(bst[:, k, a, :], src[:, a, :]).then_inc(stats_ready[k], 1)
                v.wait_ge(stats_ready[k], 4 * i + 4)
                v.nop(nofuse=True)
                for a in range(TT):
                    ins = V.bn_aggr(bag[:, k, a, :], bst[:, k, a, :]).then_inc(moments_ready[k], 1)
                v.wait_ge(moments_ready[k], 4 * i + 4)
                V.tensor_scalar(var[:, k, :], bag[:, k, :, 1], EPS, None, ALU.add).then_inc(variance_ready[k], 1)
                yield at + 3
                v.wait_ge(rstd_ready[k], i + 1)
                for a in range(TT):
                    V.tensor_scalar(dst[:, a, :], src[:, a, :], bag[:, k, a, 0:1], rs[:, k, a:a + 1],
                                    ALU.subtract, ALU.mult).then_inc(normed[k], 1)

            def pre_a(t):
                i = t.b + 1
                yield LN_AT[0]
                v.wait_ge(x_in, 16 * i + 16)
                if not known(i, 1):
                    v.wait_ge(res_ready, 2 * i)
                yield from layer_norm(0, i, LN_AT[0], xnew, xn)
                for m in range(4):
                    yield SLOT[f"in{m}"] + 2
                    v.wait_ge(tanh_ready, 4 * i + m + 1)
                    v.wait_ge(drained[BANK[f"in{m}"]], t.before(f"in{m}") + 1)
                    dst = xs[:, m, :] if m < 2 else sres[:, m - 2, :]
                    V.scalar_tensor_tensor(dst, th[:, m % 2, :], 1.0, vh[:, m % 2, :], ALU.add, ALU.mult).then_inc(silu_ready, 1)
                for m in range(2):
                    yield SLOT[f"dt{m}"] + 2
                    p = got(t, f"dt{m}")
                    v.wait_ge(abs_ready, 2 * i + m + 1)
                    if m == 0 and not known(i, 1):
                        v.wait_ge(low_part_ready, 2 * i)
                    drain(f"dt{m}", V.tensor_scalar(du[:, 0, m, :], p[:, :], bdts[:, m:m + 1], 0.0, ALU.add, ALU.max))
                for half in range(2):
                    r = 2 * i + half
                    yield SLOT["dt1"] + 7 + 6 * half
                    v.wait_ge(log_ready, i + 1)
                    v.wait_ge(drained[BANK[f"dt{half}"]], t.before(f"dt{half}") + 1)
                    V.tensor_tensor(du[:, 0, half, :], du[:, 0, half, :], spa[:, half, :], ALU.add).then_inc(steps_ready, 1)
                    yield SLOT["dt1"] + 9 + 6 * half
                    v.wait_ge(high_part_ready, r + 1)
                    if not known(r, 1):
                        v.wait_ge(low_part_ready, r)
                    V.tensor_tensor(rest[:, :], du[:, 0, half, :], parts[:, 0, half, :], ALU.subtract).then_inc(rest_ready, 1)
                    yield SLOT["dt1"] + 10 + 6 * half
                    v.wait_ge(steps_ready, 4 * i + 2 * half + 1)
                    v.wait_ge(silu_ready, 4 * i + half + 1)
                    if not known(i, 1):
                        v.wait_ge(inputs_stored[half], 16 * i)
                    V.tensor_tensor(du[:, 1, half, :], du[:, 0, half, :], xs[:, half, :], ALU.mult).then_inc(steps_ready, 1)
                    yield SLOT["dt1"] + 11 + 6 * half
                    v.wait_ge(middle_part_ready, r + 1)
                    V.tensor_tensor(parts[:, 2, half, :], rest[:, :], parts[:, 1, half, :], ALU.subtract).then_inc(low_part_ready, 1)
                for m in range(2):
                    v.wait_ge(drained[BANK[f"C{m}"]], t.before(f"C{m}") + 1)
                v.sem_inc(c_ready, 1)

            def take_sums(b, half, t, at):
                yield at
                v.wait_ge(summed, PAIRS // 4 * b + HALF // 4 * (half + 1))
                v.wait_ge(gate_ready, 2 * b + half + 1)
                v.wait_ge(direct_ready, 2 * b + half + 1)
                if not known(2 * b + half, 1):
                    v.wait_ge(gated_ready, 2 * b + half)
                V.tensor_tensor(yt[:, :], ys[:, :], cg[:, half, :], ALU.mult).then_inc(ys_taken, 1)
                yield at + 1
                v.wait_ge(ys_taken, 2 * b + half + 1)
                if half == 0 and t.post:
                    v.wait_ge(filled[BANK["z"]], t.before("z") + 1)
                V.tensor_tensor(y3[:, half, :], yt[:, :], xd[:, half, :], ALU.add).then_inc(gated_ready, 1)

            def pre_b(t):
                b = t.b
                yield GATES_AT
                v.wait_ge(silu_ready, 4 * b + 4)
                for half in range(2):
                    if half:
                        yield GATES_AT + 3
                    V.scalar_tensor_tensor(xd[:, half, :], xs[:, half, :], dps_[:, half:half + 1], sres[:, half, :],
                                           ALU.mult, ALU.mult).then_inc(direct_ready, 1)

            def routing(t, m):
                c = t.b - 1
                yield SLOT[f"lg{m}"] + 1
                p = got(t, f"lg{m}")
                drain(f"lg{m}", V.tensor_copy(lg[:, :, :].rearrange("p a e -> p (a e)"), p[:, 0:TT * E]))
                v.wait_ge(drained[BANK[f"lg{m}"]], t.before(f"lg{m}") + 1)
                done = [0]
                r0 = ROUTE * (2 * c + m - 1)

                def link(ins):
                    done[0] += 1
                    ins.then_inc(routed, 1)
                    v.wait_ge(routed, r0 + done[0])

                R = lambda n: rt[:, n, :, :]
                def bc(n):
                    return rc[:, n, :].unsqueeze(2).to_broadcast([128, TT, E])
                revb = rev[:, :].unsqueeze(1).to_broadcast([128, TT, E])
                src = lg[:, :, :]
                for n in range(2):
                    link(V.tensor_reduce(rc[:, n, :], src, AX_X, ALU.max))
                    link(V.tensor_tensor(R(0), src, bc(n), ALU.is_equal))
                    link(V.tensor_tensor(R(0), R(0), revb, ALU.mult))
                    yield SLOT[f"lg{m}"] + 2 + 2 * n
                    link(V.tensor_reduce(rc[:, 2 + n, :], R(0), AX_X, ALU.max))
                    link(V.tensor_tensor(R(1 + n), R(0), bc(2 + n), ALU.is_equal))
                    if n == 0:
                        link(V.scalar_tensor_tensor(R(3), R(1), LOWEST, lg[:, :, :], ALU.mult, ALU.add))
                        src = R(3)
                        yield SLOT[f"lg{m}"] + 3
                V.tensor_tensor(rc[:, 4, :], rc[:, 1, :], rc[:, 0, :], ALU.subtract).then_inc(gap_ready, 1)
                yield SLOT[f"lg{m}"] + 6
                v.wait_ge(gap_exp_ready, 2 * c + m)
                link(V.tensor_scalar(rc[:, 6, :], rc[:, 5, :], 1.0, 2.0, ALU.add, ALU.mult))
                link(V.reciprocal(rc[:, 6, :], rc[:, 6, :]))
                link(V.tensor_tensor(rc[:, 7, :], rc[:, 6, :], rc[:, 5, :], ALU.mult))
                link(V.tensor_tensor(R(4), R(1), bc(6), ALU.mult))
                link(V.tensor_tensor(R(5), R(2), bc(7), ALU.mult))
                link(V.tensor_tensor(R(4), R(4), R(5), ALU.add))
                assert done[0] == ROUTE

            def moe_tiles(t, m):
                c = t.b - 1
                n0 = (TT - 1) * E * (2 * c + m - 1)
                for slot, name, n in moe_v(m):
                    yield slot
                    if name == "h":
                        p = got(t, f"h{m}_{n}")
                        v.wait_ge(hidden_tanh_ready, 4 * E * c + 2 * E * (m - 1) + n + 1)
                        drain(f"h{m}_{n}", V.scalar_tensor_tensor(sq[:, n % 2, :], tq[:, n % 2, :], 1.0, p[:, :],
                                                                  ALU.add, ALU.mult))
                    elif name == "g":
                        p = got(t, f"g{m}_{n}")
                        v.wait_ge(drained[BANK[f"h{m}_{n}"]], t.before(f"h{m}_{n}") + 1)
                        if n >= 4:
                            v.wait_ge(filled["Y"], t.before(f"y{m}_{n // 2 - 2}") + 1)
                        drain(f"g{m}_{n}", V.tensor_tensor(aq[:, n % 4, :], sq[:, n % 2, :], p[:, :], ALU.mult))
                    else:
                        p = got(t, f"y{m}_{n}")
                        if n >= 1:
                            v.wait_ge(added, n0 + (TT - 1) * n)
                            v.wait_ge(drained["Y"], t.before(f"y{m}_{n - 1}") + 1)
                        for a in range(TT):
                            ins = V.scalar_tensor_tensor(x1[:, a, :], p[:, a * 128:(a + 1) * 128], rt[:, 4, a, n:n + 1],
                                                         x1[:, a, :], ALU.mult, ALU.add)
                            if a < TT - 1:
                                ins.then_inc(added, 1)
                        drain(f"y{m}_{n}", ins)
                v.wait_ge(added, n0 + (TT - 1) * E)
                v.wait_ge(drained["Y"], t.before(f"y{m}_{E - 1}") + 1)

            def post(t):
                c = t.b - 1
                yield from take_sums(c, 1, t, 2)
                yield SLOT["z"] + 2
                p = got(t, "z")
                v.wait_ge(res_ready, 2 * c + 2)
                drain("z", V.tensor_tensor(z[:, :, :].rearrange("p a c -> p (a c)"), p[:, :],
                                           resa[:, :, :].rearrange("p a c -> p (a c)"), ALU.add))
                v.wait_ge(drained[BANK["z"]], t.before("z") + 1)
                yield from layer_norm(1, c, LN_AT[1], z, nrm)
                yield LN_AT[1] + 4
                v.wait_ge(normed[1], 4 * c + 4)
                V.tensor_tensor(nrm[:, :, :], nrm[:, :, :], bcs[:, 1:2, :].to_broadcast([128, TT, D]), ALU.mult).then_inc(scaled_ready, 1)
                yield LN_AT[1] + 4
                v.wait_ge(scaled_ready, c + 1)
                v.wait_ge(x_out, 16 * c + 16)
                V.tensor_tensor(x1[:, :, :], nrm[:, :, :], resb[:, :, :], ALU.add).then_inc(x1_ready, 1)
                v.wait_ge(x1_ready, c + 1)
                yield from layer_norm(2, c, LN_AT[2], x1, nrm)
                yield from both(moe_tiles(t, 1), routing(t, 1))
                flat = lambda ap: ap[:, :, :].rearrange("p a c -> p (a c)")
                yield from layer_norm(3, c, LN_AT[3], x1, nrm)
                yield SLOT["P1"] + 1
                p1, p2 = got(t, "P1"), got(t, "P2")
                drain("P1", V.tensor_tensor(zt[2], p1[:, :], cosT[:, :], ALU.mult))
                drain("P2", V.tensor_tensor(zt[3], p2[:, :], sinT[:, :], ALU.mult))
                yield SLOT["P1"] + 2
                v.wait_ge(drained[BANK["P1"]], t.before("P1") + 1)
                v.wait_ge(drained[BANK["P2"]], t.before("P2") + 1)
                V.tensor_tensor(zt[2], zt[2], zt[3], ALU.add).then_inc(turned_ready, 1)
                yield SLOT["P1"] + 3
                v.wait_ge(turned_ready, c + 1)
                V.tensor_tensor_scan(zt[3], rT[:, :], zt[2], 0.0, ALU.mult, ALU.add).then_inc(diagonal_scanned, 1)
                yield SLOT["P1"] + 4
                v.wait_ge(diagonal_scanned, c + 1)
                V.tensor_tensor(zt[0], zt[3], cosT[:, :], ALU.mult).then_inc(real_ready, 1)
                yield SLOT["P1"] + 5
                V.tensor_tensor(zt[1], zt[3], sinT[:, :], ALU.mult).then_inc(imaginary_ready, 1)
                yield SLOT["s5"] + 1
                p = got(t, "s5")
                drain("s5", V.scalar_tensor_tensor(yT[:, :], nT[:, :], sdt[:, 0:1], p[:, :], ALU.mult, ALU.add))
                yield SLOT["s5t"] + 1
                p = got(t, "s5t")
                drain("s5t", V.tensor_tensor(flat(x1), flat(x1), p[:, :], ALU.add))
                v.wait_ge(drained[BANK["s5t"]], t.before("s5t") + 1)
                yield from layer_norm(4, c, LN_AT[4], x1, nrm)
                yield from both(moe_tiles(t, 2), routing(t, 2))
                v.sem_inc(sequence_done, 1)

            def scan(t):
                K = PAIRS * t.b

                def pair(k):
                    v.wait_ge(decay_ready, K + k + 1)
                    v.wait_ge(product_ready, K + k + 1)
                    if not known(K + k, H_RING):
                        v.wait_ge(summed, (PAIRS // 4) * t.b + (k - H_RING) // 4 + 1)
                    V.tensor_tensor_scan(h[:, k % H_RING, :], dtp[k % D_RING][:, :], w[:, k % W_RING, :], 0.0,
                                         ALU.mult, ALU.add).then_inc(scanned, 1)

                weave(pair, [pre_b(t), take_sums(t.b, 0, t, HALF + SUM_AT - 1)]
                      + tasks_of(t, pre_a, post, [diagonal_setup()] if known(t.b, 1) else []))

            turns(v, pre_a, scan, post)


_INS = ['L0_attn_a_x', 'L0_attn_a_Wi', 'L0_attn_a_bi', 'L0_attn_a_Wx', 'L0_attn_a_bx', 'L0_attn_a_Wdt', 'L0_attn_a_bdt',
        'L0_attn_a_A_log', 'L0_attn_a_Dp', 'L0_attn_a_Wo', 'L0_attn_a_bo', 'L0_attn_a_gamma', 'L0_attn_a_beta',
        'L0_attn_b_Lambda_re', 'L0_attn_b_Lambda_im', 'L0_attn_b_B', 'L0_attn_b_C', 'L0_attn_b_D', 'L0_attn_b_log_step',
        'L0_ffn_Wg', 'L0_ffn_W1', 'L0_ffn_W2', 'L0_ffn_W3']


def kernel(**inputs):
    import ml_dtypes
    import numpy as _np
    import concourse.bacc as _bacc
    from concourse import mybir as _mybir
    from concourse.bass_utils import run_bass_kernel_spmd as _run

    i, r, col = _np.arange(16)[None, :, None], _np.arange(96)[:, None, None] % 32, _np.arange(128)[None, None, :]
    sel = (r == 2 * i + col // 64).astype(ml_dtypes.bfloat16).reshape(96, 16 * 128)
    p, c32 = _np.arange(128)[:, None, None], _np.arange(32)[None, None, :]
    wsum = (c32 == 2 * i + p // 64).astype(_np.float32).reshape(128, 16 * 32)
    rev = _np.broadcast_to(8.0 - _np.arange(8), (128, 8)).astype(_np.float32)
    constants = {"c_ident": _np.eye(128, dtype=_np.float32), "c_sel": sel, "c_wsum": wsum, "c_rev": rev}

    nc = _bacc.Bacc("TRN2", target_bir_lowering=False, num_devices=1)
    arrays, args = {}, []
    for name, a in [(n, inputs[n]) for n in _INS] + list(constants.items()):
        a = _np.ascontiguousarray(a)
        arrays[f"in_{name}_dram"] = a
        args.append(nc.dram_tensor(f"in_{name}_dram", a.shape, _mybir.dt.from_np(a.dtype), kind="ExternalInput").ap())
    args.append(nc.dram_tensor("u_rows", (8, 256, 512), _mybir.dt.float32, kind="Internal").ap())
    args.append(nc.dram_tensor("out_0_dram", (8, 512, 128), _mybir.dt.float32, kind="ExternalOutput").ap())
    hybrid_kernel(nc, *args)
    r = _run(nc, [arrays], core_ids=[0])
    return r.results[0]["out_0_dram"]
```
